# Optimizing a Trainium2 kernel written in Bass

```python
import numpy as np
import jax
import jax.numpy as jnp

def _softmax(x, axis=-1):
    return jax.nn.softmax(x, axis=axis)

def _gelu(x):
    return jax.nn.gelu(x, approximate=True)

def _silu(x):
    return jax.nn.silu(x)

def _sigmoid(x):
    return jax.nn.sigmoid(x)

def _layernorm(x, axis=-1, eps=1e-05):
    m = jnp.mean(x, axis=axis, keepdims=True)
    v = jnp.var(x, axis=axis, keepdims=True)
    return (x - m) / jnp.sqrt(v + eps)

def _scatter_add(tgt, idx, src, axis=0):
    return tgt.at[idx].add(src)

def _segment_sum(src, seg, n):
    return jax.ops.segment_sum(src, seg, n)
kernel_name = 'mk_prb_d1_jaxref_r2_cbaa89'

def setup_inputs(seed: int=0):
    np.random.seed(seed)
    _w = jnp.asarray

    def _L0_attn_setup():
        import jax, jax.numpy as jnp
        import numpy as np
        import math
        D_MODEL = 512
        NUM_HEADS = 16
        D_HEAD = D_MODEL // NUM_HEADS
        N_FREQ = D_HEAD // 2 + 1
        COMPRESSION_RATIO = 0.5

        def _spectral_filter(t, mask):
            tf = jnp.fft.rfft(t, axis=-1)
            tf = tf * mask
            return jnp.fft.irfft(tf, n=t.shape[-1], axis=-1).astype(t.dtype)
        key = jax.random.key(seed)
        k_x, k_qkv, k_out, k_b, k_m = jax.random.split(key, 5)
        B, S = (2, 1024)
        x = jax.random.normal(k_x, (B, S, D_MODEL), dtype=jnp.float32)
        w_qkv = jax.random.normal(k_qkv, (D_MODEL, 3 * D_MODEL), dtype=jnp.float32) / math.sqrt(D_MODEL)
        w_out = jax.random.normal(k_out, (D_MODEL, D_MODEL), dtype=jnp.float32) / math.sqrt(D_MODEL)
        b_out = jax.random.normal(k_b, (D_MODEL,), dtype=jnp.float32) * 0.01
        init_logit = math.log(COMPRESSION_RATIO / (1.0 - COMPRESSION_RATIO))
        mask_logits = init_logit + 0.1 * jax.random.normal(k_m, (N_FREQ,), dtype=jnp.float32)
        return {'x': x, 'w_qkv': w_qkv, 'w_out': w_out, 'b_out': b_out, 'mask_logits': mask_logits}
    _L0_attn_in = _L0_attn_setup()

    def _L0_ffn_setup():
        import jax, jax.numpy as jnp
        import numpy as np
        EXPERT_NUM = 8
        CAPACITY = 100
        key = jax.random.key(seed)
        k1, k2, k3 = jax.random.split(key, 3)
        B, S, H, E = (8, 1024, 512, EXPERT_NUM)
        x = jax.random.normal(k1, (B, S, H), dtype=jnp.float32)
        w_gate = jax.random.normal(k2, (H, E), dtype=jnp.float32) * 0.02
        w_expert = jax.random.normal(k3, (H, H), dtype=jnp.float32) * 0.02
        b_expert = jnp.zeros((H,), dtype=jnp.float32)
        return {'x': x, 'w_gate': w_gate, 'w_expert': w_expert, 'b_expert': b_expert}
    _L0_ffn_in = _L0_ffn_setup()
    _d = {'L0_attn_x': _L0_attn_in['x'], 'L0_attn_w_qkv': _L0_attn_in['w_qkv'], 'L0_attn_w_out': _L0_attn_in['w_out'], 'L0_attn_b_out': _L0_attn_in['b_out'], 'L0_attn_mask_logits': _L0_attn_in['mask_logits'], 'L0_ffn_w_gate': _L0_ffn_in['w_gate'], 'L0_ffn_w_expert': _L0_ffn_in['w_expert'], 'L0_ffn_b_expert': _L0_ffn_in['b_expert']}
    _x0 = _d['L0_attn_x']
    _d['L0_attn_x'] = jax.random.normal(jax.random.fold_in(jax.random.key(seed), 1), (4, 2048, 512), dtype=_x0.dtype)
    del _x0
    return _d

def reference(L0_attn_x, L0_attn_w_qkv, L0_attn_w_out, L0_attn_b_out, L0_attn_mask_logits, L0_ffn_w_gate, L0_ffn_w_expert, L0_ffn_b_expert):

    def _L0_attn_ref(x, w_qkv, w_out, b_out, mask_logits):
        import jax, jax.numpy as jnp
        import numpy as np
        import math
        D_MODEL = 512
        NUM_HEADS = 16
        D_HEAD = D_MODEL // NUM_HEADS
        N_FREQ = D_HEAD // 2 + 1
        COMPRESSION_RATIO = 0.5

        def _spectral_filter(t, mask):
            tf = jnp.fft.rfft(t, axis=-1)
            tf = tf * mask
            return jnp.fft.irfft(tf, n=t.shape[-1], axis=-1).astype(t.dtype)
        B, S, D = x.shape
        H, dh = (NUM_HEADS, D_HEAD)
        qkv = x @ w_qkv
        q, k, v = jnp.split(qkv, 3, axis=-1)
        to_heads = lambda t: t.reshape(B, S, H, dh).transpose(0, 2, 1, 3)
        q, k, v = (to_heads(q), to_heads(k), to_heads(v))
        mask = jax.nn.sigmoid(mask_logits)
        q = _spectral_filter(q, mask)
        k = _spectral_filter(k, mask)
        scores = jnp.einsum('bhqd,bhkd->bhqk', q, k) / math.sqrt(dh)
        attn = jax.nn.softmax(scores, axis=-1)
        out = jnp.einsum('bhqk,bhkd->bhqd', attn, v)
        out = out.transpose(0, 2, 1, 3).reshape(B, S, D)
        return out @ w_out + b_out

    def _L0_ffn_ref(x, w_gate, w_expert, b_expert):
        import jax, jax.numpy as jnp
        import numpy as np
        EXPERT_NUM = 8
        CAPACITY = 100
        B, S, H = x.shape
        E, C = (EXPERT_NUM, CAPACITY)
        hs = x.reshape(-1, H)
        logits = hs @ w_gate
        probs = jax.nn.softmax(logits, axis=1)
        best = jnp.argmax(probs, axis=1)
        mask = jax.nn.one_hot(best, E, dtype=jnp.int32)
        gate = jnp.sum(probs * mask.astype(probs.dtype), axis=1)
        locations = jnp.cumsum(mask, axis=0) - 1
        mask = mask * (locations < C).astype(jnp.int32)
        loc_sum = jnp.sum(locations * mask, axis=1)
        new_gates = gate[:, None] * mask.astype(probs.dtype)
        loc_oh = jax.nn.one_hot(loc_sum, C, dtype=probs.dtype)
        combine = new_gates[:, :, None] * loc_oh[:, None, :]
        dispatch = (combine != 0).astype(hs.dtype)
        dispatched = jnp.einsum('tec,th->ech', dispatch, hs).reshape(E * C, H)
        expert_out = dispatched @ w_expert + b_expert
        combined = combine.reshape(-1, E * C) @ expert_out
        return combined.reshape(B, S, H)
    x = L0_attn_x
    xn = _layernorm(x, axis=-1)
    x = x + _L0_attn_ref(xn, L0_attn_w_qkv, L0_attn_w_out, L0_attn_b_out, L0_attn_mask_logits) + _L0_ffn_ref(xn, L0_ffn_w_gate, L0_ffn_w_expert, L0_ffn_b_expert)
    return x

_drawn_inputs = setup_inputs


def setup_inputs(seed=0):
    import zlib

    import numpy as np

    out = dict(_drawn_inputs(seed))
    spreads = {'L0_ffn_b_expert': (0.0, 0.8)}
    factors = {'L0_attn_b_out': 6.026, 'L0_attn_mask_logits': 49.429, 'L0_ffn_w_gate': 6.028}
    for name, (base, spread) in spreads.items():
        noise = np.random.default_rng([zlib.crc32(name.encode()), seed]).standard_normal(out[name].shape)
        drawn = base * np.exp(spread * noise) if base else spread * noise
        out[name] = jnp.asarray(drawn.astype(out[name].dtype))
    for name, factor in factors.items():
        out[name] = (out[name] * factor).astype(out[name].dtype)
    return out
```

```python
from contextlib import ExitStack

import concourse.bass as bass
from concourse import mybir

F32 = mybir.dt.float32
F16 = mybir.dt.float16
BF16 = mybir.dt.bfloat16
ALU = mybir.AluOpType
ACT = mybir.ActivationFunctionType
AX = mybir.AxisListType

P = 128
CH = 512
EXPERTS = 8
CAPACITY = 100
EPS = 1e-5
MSCALE = 256.0


def attention_and_experts_kernel(nc, x, w_qkv, w_out, b_out, mask_logits, w_gate, w_expert, b_expert,
                                 ident_c, basis_c, prefix_c, rank_c, out):
    B, S, D = x.shape
    DH = 32
    NF = mask_logits.shape[0]
    HQ = P // DH
    QUADS = D // P
    KB = D // P
    TT = CH // P
    CPB = S // CH
    NCH = B * CPB
    QB = B * QUADS
    NT = B * S // P
    STEPS = S // P
    UNITS = QB * CPB
    SCALE = float(DH) ** -0.5
    assert D == CH and DH == 32 and NF == DH // 2 + 1

    x_rows = x.rearrange("b s d -> (b s) d")
    out_rows = out.rearrange("b s d -> (b s) d")
    qk_dram = nc.dram_tensor("qk_scratch", (QB, 2, CPB, 2, P, CH), F16).ap()
    v_dram = nc.dram_tensor("v_scratch", (QB, CPB, P, TT, P), F32).ap()
    y_dram = nc.dram_tensor("y_scratch", (B * S, D), F32).ap()
    a_dram = nc.dram_tensor("attn_scratch", (UNITS, P, CH), F32).ap()

    with ExitStack() as whole:
        def keep(name, shape, dt):
            return whole.enter_context(nc.sbuf_tensor(name, shape, dt))

        ident = keep("ident", [P, P], F32)
        w_out_sb = keep("w_out_sb", [P, QUADS, D], F32)
        b_out_sb = keep("b_out_sb", [P, D], F32)
        logits = keep("logits", [P, NT, EXPERTS], F32)
        gate = keep("gate", [P, NT], F32)

        project(nc, locals())
        route(nc, locals())
        attend(nc, locals())
        finish_rows(nc, locals())


def project(nc, g):
    D, DH, NF, HQ, QUADS, KB, TT, CPB, NCH = (g[k] for k in ("D", "DH", "NF", "HQ", "QUADS", "KB", "TT", "CPB", "NCH"))
    B = g["B"]
    ident, logits = g["ident"], g["logits"]
    MB = 2 * D // P
    QK_RING, V_RING, Y_RING, MM_RING = 4, 2, 2, 4
    GROUPS = MB + 2 * TT

    with ExitStack() as ctx:
        def sb(name, shape, dt):
            return ctx.enter_context(nc.sbuf_tensor(name, shape, dt))

        def pb(name, shape, dt):
            return ctx.enter_context(nc.psum_tensor(name, shape, dt))

        def sem(name):
            return ctx.enter_context(nc.semaphore(name))

        w_qkv_sb = sb("w_qkv_sb", [P, KB, 3 * D], F32)
        w_filt = sb("w_filt", [P, KB, 2 * D], F32)
        w_exp_sb = sb("w_exp_sb", [P, KB, D], F32)
        w_gate_sb = sb("w_gate_sb", [P, KB, DH], F32)
        b_exp_sb = sb("b_exp_sb", [P, D], F32)
        basis = sb("basis", [P, P], F32)
        basis_m = sb("basis_m", [P, P], F32)
        filt = sb("filt", [P, P], F32)
        mask = sb("mask", [P, 3], F32)
        eps = sb("eps", [P, 1], F32)
        wt = sb("wt", [P, 2, D], F32)
        xs = sb("xs", [P, 2, TT, D], F32)
        xt = sb("xt", [P, 2, KB, CH], F32)
        stats = sb("stats", [P, TT, 6], F32)
        mean_var = sb("mean_var", [P, TT, 2], F32)
        std = sb("std", [P, TT], F32)
        rstd = sb("rstd", [P, TT], F32)
        qk_out = sb("qk_out", [P, QK_RING, 2, CH], F16)
        v_out = sb("v_out", [P, V_RING, D], F32)
        y_out = sb("y_out", [P, Y_RING, D], F32)
        lg_sb = sb("lg_sb", [P, CH], F32)

        mm = [pb(f"mm{i}", [P, CH], F32) for i in range(MM_RING)]
        xt_ps = [pb(f"xt_ps{i}", [P, CH], F32) for i in range(2)]
        lg_ps = pb("lg_ps", [P, CH], F32)
        lt_ps = pb("lt_ps", [P, CH], F32)

        weights_in = sem("weights_in")
        zeroed = sem("zeroed")
        mask_exp = sem("mask_exp")
        mask_step = sem("mask_step")
        basis_ready = sem("basis_ready")
        filt_made = sem("filt_made")
        filt_ready = sem("filt_ready")
        wt_made = sem("wt_made")
        wt_ready = sem("wt_ready")
        wf_made = sem("wf_made")
        wf_ready = sem("wf_ready")

        with nc.Block() as block:
            @block.sync
            def _(sp):
                n = 0
                view = mask[:, 0:1]
                ml = g["mask_logits"].rearrange("(f o) -> f o", o=1)
                loads = [
                    (w_qkv_sb[:, :, :], g["w_qkv"].rearrange("(j p) n -> p j n", p=P)),
                    (ident[:, :], g["ident_c"]), (basis[:, :], g["basis_c"]),
                    (w_exp_sb[:, :, :], g["w_expert"].rearrange("(j p) n -> p j n", p=P)),
                    (b_exp_sb[:, :], g["b_expert"].partition_broadcast(P)),
                    (g["b_out_sb"][:, :], g["b_out"].partition_broadcast(P)),
                    (g["w_out_sb"][:, :, :], g["w_out"].rearrange("(j p) n -> p j n", p=P)),
                ]
                for h in range(HQ):
                    loads.append((view[h * DH:h * DH + NF, :], ml))
                    loads.append((view[h * DH + NF:(h + 1) * DH, :], ml[1:NF - 1, :]))
                for dst, src in loads:
                    sp.dma_start(dst, src).then_inc(weights_in, 16)
                    n += 16
                sp.wait_ge(zeroed, 1)
                sp.dma_start(w_gate_sb[:, :, 0:EXPERTS], g["w_gate"].rearrange("(j p) n -> p j n", p=P)).then_inc(weights_in, 16)
                sp.wait_ge(weights_in, n + 16)

            n_loads = 7 + 2 * HQ + 1

            @block.scalar
            def _(act):
                act.wait_ge(weights_in, 16 * n_loads)
                nc.scalar.activation(mask[:, 1:2], mask[:, 0:1], ACT.Exp, scale=-1.0).then_inc(mask_exp, 1)
                for m in range(MB):
                    act.wait_ge(wf_made, m + 1)
                    nc.scalar.activation(w_filt[:, :, m * P:(m + 1) * P],
                                         mm[m % 2][:, :].rearrange("p (j n) -> p j n", j=KB), ACT.Copy).then_inc(wf_ready, 1)

            @block.vector
            def _(dve):
                nc.vector.memset(w_gate_sb[:, :, :], 0.0).then_inc(zeroed, 1)
                nc.vector.memset(eps[:, :], EPS)
                dve.wait_ge(mask_exp, 1)
                nc.vector.tensor_scalar_add(mask[:, 2:3], mask[:, 1:2], 1.0).then_inc(mask_step, 1)
                dve.wait_ge(mask_step, 1)
                nc.vector.reciprocal(mask[:, 1:2], mask[:, 2:3]).then_inc(mask_step, 1)
                dve.wait_ge(mask_step, 2)
                nc.vector.tensor_scalar(basis_m[:, :], basis[:, :], mask[:, 1:2], None, ALU.mult).then_inc(basis_ready, 1)
                dve.wait_ge(filt_made, 1)
                nc.vector.tensor_copy(filt[:, :], lg_ps[:, 0:P]).then_inc(filt_ready, 1)
                for m in range(MB):
                    dve.wait_ge(wt_made, m + 1)
                    if m >= 2:
                        dve.wait_ge(wf_made, m - 1)
                    nc.vector.tensor_copy(wt[:, m % 2, :], xt_ps[m % 2][:, :]).then_inc(wt_ready, 1)

            @block.tensor
            def _(pe):
                pe.wait_ge(weights_in, 16 * n_loads)
                pe.wait_ge(basis_ready, 1)
                nc.tensor.matmul(lg_ps[:, 0:P], basis_m[:, :], basis[:, :], start=True, stop=True).then_inc(filt_made, 1)

                def turn(m):
                    if m >= 2:
                        pe.wait_ge(wt_ready, m - 1)
                    for j in range(KB):
                        last = nc.tensor.transpose(xt_ps[m % 2][:, j * P:(j + 1) * P], w_qkv_sb[:, j, m * P:(m + 1) * P], ident[:, :])
                    last.then_inc(wt_made, 1)

                turn(0)
                pe.wait_ge(filt_ready, 1)
                for m in range(MB):
                    if m + 1 < MB:
                        turn(m + 1)
                    pe.wait_ge(wt_ready, m + 1)
                    if m >= 2:
                        pe.wait_ge(wf_ready, m - 1)
                    for j in range(KB):
                        last = nc.tensor.matmul(mm[m % 2][:, j * P:(j + 1) * P], wt[:, m % 2, j * P:(j + 1) * P], filt[:, :],
                                                start=True, stop=True, skip_group_check=True)
                    last.then_inc(wf_made, 1)

        x_in = [sem(f"x_in{u}") for u in range(2)]
        x_turned = sem("x_turned")
        varied = sem("varied")
        stats_seen = sem("stats_seen")
        aggregated = sem("aggregated")
        std_ready = sem("std_ready")
        rstd_ready = sem("rstd_ready")
        xn_ready = sem("xn_ready")
        xt_made = sem("xt_made")
        xt_ready = sem("xt_ready")
        lg_made = sem("lg_made")
        lg_ready = sem("lg_ready")
        lt_made = sem("lt_made")
        lt_summed = sem("lt_summed")
        mm_done = sem("mm_done")
        hi_ready = sem("hi_ready")
        lo_ready = sem("lo_ready")
        v_ready = sem("v_ready")
        y_ready = sem("y_ready")
        qk_stored = [sem(f"qk_stored{i}") for i in range(QK_RING)]
        v_stored = [sem(f"v_stored{i}") for i in range(V_RING)]
        y_stored = [sem(f"y_stored{i}") for i in range(Y_RING)]
        PAIRS = NCH // 2

        with nc.Block() as block:
            @block.gpsimd
            def _(pool):
                with pool.Fori(0, PAIRS) as i:
                    for u in range(2):
                        pool.wait_ge(x_turned, i * 2 + (u + 1))
                        nc.gpsimd.dma_start(xs[:, u, :, :],
                                            g["x_rows"].rearrange("(i u t p) d -> i u p t d", u=2, t=TT, p=P)[i, u]).then_inc(x_in[u], 16)

            @block.sync
            def _(sp):
                for s in (*qk_stored, *v_stored, *y_stored):
                    sp.sem_inc(s, 16)
                y_view = g["y_dram"].rearrange("(b c t p) d -> b c t p d", b=B, c=CPB, t=TT)
                with sp.Fori(0, B) as b:
                    with sp.Fori(0, CPB // 2) as ci:
                        for u in range(2):
                            c = b * CPB + ci * 2 + u
                            ch = ci * 2 + u
                            for m in range(MB):
                                sp.wait_ge(lo_ready, c * MB + (m + 1))
                                dst = g["qk_dram"].rearrange("(b q) k c l p t -> b q k c p l t", b=B)[b, m % QUADS, m // QUADS, ch]
                                sp.dma_start(dst, qk_out[:, m % QK_RING, :, :]).then_inc(qk_stored[m % QK_RING], 16)
                            for t in range(TT):
                                sp.wait_ge(v_ready, c * TT + (t + 1))
                                dst = g["v_dram"].rearrange("(b q) c p t n -> b c t p q n", b=B)[b, ch, t]
                                sp.dma_start(dst, v_out[:, t % V_RING, :].rearrange("p (q n) -> p q n", q=QUADS)).then_inc(v_stored[t % V_RING], 16)
                            for t in range(TT):
                                sp.wait_ge(y_ready, c * TT + (t + 1 + TT))
                                sp.dma_start(y_view[b, ch, t], y_out[:, t % Y_RING, :]).then_inc(y_stored[t % Y_RING], 16)
                for s in qk_stored:
                    sp.wait_ge(s, 16 * (1 + NCH * MB // QK_RING))
                for s in v_stored:
                    sp.wait_ge(s, 16 * (1 + NCH * TT // V_RING))
                for s in y_stored:
                    sp.wait_ge(s, 16 * (1 + NCH * TT // Y_RING))

            @block.scalar
            def _(act):
                act.sem_inc(xt_ready, 2)
                act.sem_inc(lg_ready, 1)

                def deviation(c):
                    act.wait_ge(aggregated, c + 1)
                    nc.scalar.activation(std[:, :], mean_var[:, :, 1], ACT.Sqrt, bias=eps[:, 0:1]).then_inc(std_ready, 1)

                def turned(c, u):
                    for j in range(KB):
                        act.wait_ge(xt_made, c * KB + (j + 1))
                        nc.scalar.activation(xt[:, u, j, :], xt_ps[j % 2][:, :], ACT.Copy).then_inc(xt_ready, 1)

                def chunk(c, u, more):
                    act.wait_ge(lg_made, c + 1)
                    act.wait_ge(lt_made, c + 1)
                    nc.scalar.activation(lg_sb[:, :], lg_ps[:, :], ACT.Copy).then_inc(lg_ready, 1)
                    for m in range(MB):
                        act.wait_ge(mm_done, c * GROUPS + (m + 1))
                        act.wait_ge(qk_stored[m % QK_RING], (c * (MB // QK_RING) + (m // QK_RING + 1)) * 16)
                        nc.scalar.activation(qk_out[:, m % QK_RING, 0, :], mm[m % MM_RING][:, :], ACT.Copy).then_inc(hi_ready, 1)
                        if m == 5 and more:
                            deviation(c + 1)
                    if more:
                        turned(c + 1, 1 - u)
                    for t in range(TT):
                        act.wait_ge(mm_done, c * GROUPS + (MB + t + 1))
                        act.wait_ge(v_stored[t % V_RING], (c * (TT // V_RING) + (t // V_RING + 1)) * 16)
                        nc.scalar.activation(v_out[:, t % V_RING, :], mm[(MB + t) % MM_RING][:, :], ACT.Copy).then_inc(v_ready, 1)

                deviation(0)
                turned(0, 0)
                with act.Fori(0, PAIRS - 1) as i:
                    chunk(i * 2, 0, True)
                    chunk(i * 2 + 1, 1, True)
                chunk(NCH - 2, 0, True)
                chunk(NCH - 1, 1, False)

            @block.vector
            def _(dve):
                dve.sem_inc(y_ready, TT)
                dve.sem_inc(lt_summed, 1)

                def moments(c, c2, u):
                    dve.wait_ge(x_in[u], (c2 + 1) * 16)
                    for t in range(TT):
                        last = nc.vector.bn_stats(stats[:, t, :], xs[:, u, t, :])
                    last.then_inc(varied, 1)
                    dve.wait_ge(varied, c + 1)
                    dve.sem_inc(stats_seen, 1)
                    for t in range(TT):
                        last = nc.vector.bn_aggr(mean_var[:, t, :], stats[:, t, :])
                    last.then_inc(aggregated, 1)

                def normalise(c, u):
                    dve.wait_ge(std_ready, c + 1)
                    nc.vector.reciprocal(rstd[:, :], std[:, :]).then_inc(rstd_ready, 1)
                    dve.wait_ge(rstd_ready, c + 1)
                    for t in range(TT):
                        last = nc.vector.tensor_scalar(xs[:, u, t, :], xs[:, u, t, :], mean_var[:, t, 0:1], rstd[:, t:t + 1],
                                                       ALU.subtract, ALU.mult)
                    last.then_inc(xn_ready, 1)

                def chunk(c, c2, u, more):
                    for m in range(MB):
                        dve.wait_ge(hi_ready, c * MB + (m + 1))
                        nc.vector.tensor_tensor(qk_out[:, m % QK_RING, 1, :], mm[m % MM_RING][:, :], qk_out[:, m % QK_RING, 0, :],
                                                ALU.subtract).then_inc(lo_ready, 1)
                        if m == 3 and more:
                            moments(c + 1, c2 + u, 1 - u)
                        if m == 5 and more:
                            normalise(c + 1, 1 - u)
                    dve.wait_ge(lt_made, c + 2)
                    nc.vector.tensor_reduce(out=logits[:, bass.ds(c * TT, TT), :],
                                            in_=lt_ps[:, :].rearrange("p (t j e) -> p t e j", t=TT, j=KB)[:, :, 0:EXPERTS, :],
                                            op=ALU.add, axis=AX.X).then_inc(lt_summed, 1)
                    for t in range(TT):
                        dve.wait_ge(mm_done, c * GROUPS + (MB + TT + t + 1))
                        dve.wait_ge(y_stored[t % Y_RING], (c * (TT // Y_RING) + (t // Y_RING + 1)) * 16)
                        nc.vector.tensor_tensor(y_out[:, t % Y_RING, :], mm[(MB + TT + t) % MM_RING][:, :], b_exp_sb[:, :],
                                                ALU.add).then_inc(y_ready, 1)

                moments(0, 0, 0)
                normalise(0, 0)
                with dve.Fori(0, PAIRS - 1) as i:
                    chunk(i * 2, i, 0, True)
                    chunk(i * 2 + 1, i, 1, True)
                chunk(NCH - 2, PAIRS - 1, 0, True)
                chunk(NCH - 1, PAIRS - 1, 1, False)

            @block.tensor
            def _(pe):
                pe.sem_inc(x_turned, 2)
                pe.sem_inc(lt_made, 1)

                def turn(c, u):
                    pe.wait_ge(xn_ready, c + 1)
                    for j in range(KB):
                        pe.wait_ge(xt_ready, c * KB + (j + 1))
                        for t in range(TT):
                            last = nc.tensor.transpose(xt_ps[j % 2][:, t * P:(t + 1) * P], xs[:, u, t, j * P:(j + 1) * P], ident[:, :])
                        last.then_inc(xt_made, 1)
                    pe.wait_ge(xt_ready, c * KB + (KB + 2))
                    pe.sem_inc(x_turned, 1)

                def group(c, n, lhs, rhs):
                    if n < TT:
                        pe.wait_ge(y_ready, c * TT + (n + 1))
                    elif n < MB + TT:
                        pe.wait_ge(lo_ready, c * MB + (n - MM_RING + 1))
                    else:
                        pe.wait_ge(v_ready, c * TT + (n - MB - TT + 1))
                    for j in range(KB):
                        last = nc.tensor.matmul(mm[n % MM_RING][:, :], lhs(j), rhs(j), start=(j == 0), stop=(j == KB - 1))
                    last.then_inc(mm_done, 1)

                def chunk(c, u, more):
                    pe.wait_ge(xt_ready, c * KB + (KB + 2))
                    pe.wait_ge(lg_ready, c + 1)
                    for j in range(KB):
                        last = nc.tensor.matmul(lg_ps[j * DH:(j + 1) * DH, :], w_gate_sb[:, j, :], xt[:, u, j, :], start=True, stop=True)
                    last.then_inc(lg_made, 1)
                    for m in range(MB):
                        group(c, m, lambda j: w_filt[:, j, m * P:(m + 1) * P], lambda j: xt[:, u, j, :])
                    if more:
                        turn(c + 1, 1 - u)
                    for t in range(TT):
                        group(c, MB + t, lambda j: xt[:, u, j, t * P:(t + 1) * P], lambda j: w_qkv_sb[:, j, 2 * D:3 * D])
                    pe.wait_ge(lg_ready, c + 2)
                    pe.wait_ge(lt_summed, c + 1)
                    for t in range(TT):
                        last = nc.tensor.transpose(lt_ps[:, t * P:(t + 1) * P], lg_sb[:, t * P:(t + 1) * P], ident[:, :])
                    last.then_inc(lt_made, 1)
                    for t in range(TT):
                        group(c, MB + TT + t, lambda j: xt[:, u, j, t * P:(t + 1) * P], lambda j: w_exp_sb[:, j, :])

                turn(0, 0)
                with pe.Fori(0, PAIRS - 1) as i:
                    chunk(i * 2, 0, True)
                    chunk(i * 2 + 1, 1, True)
                chunk(NCH - 2, 0, True)
                chunk(NCH - 1, 1, False)


def route(nc, g):
    NT = g["NT"]
    logits, gate = g["logits"], g["gate"]
    with ExitStack() as ctx:
        def sb(name, shape, dt):
            return ctx.enter_context(nc.sbuf_tensor(name, shape, dt))

        shape = [P, NT, EXPERTS]
        probs = sb("gate_probs", shape, F32)
        work = sb("work", shape, F32)
        onehot = sb("onehot", shape, F32)
        onehot16 = sb("onehot16", shape, BF16)
        totals = sb("totals", shape, F32)
        places = sb("places", shape, F32)
        ones_row = sb("ones_row", [P, NT], F32)
        prefix = sb("prefix", [P, P], F32)
        prefix16 = sb("prefix16", [P, P], BF16)
        all16 = sb("all16", [P, P], BF16)
        rank = sb("rank", [P, EXPERTS], F32)
        top = sb("top", [P, NT], F32)
        total = sb("total", [P, NT], F32)
        first = sb("first", [P, NT], F32)
        taken = sb("taken", [P, NT], F32)
        here_ps = ctx.enter_context(nc.psum_tensor("here_ps", [P, NT * EXPERTS], F32))
        all_ps = ctx.enter_context(nc.psum_tensor("all_ps", [P, NT * EXPERTS], F32))
        consts_in = ctx.enter_context(nc.semaphore("consts_in"))
        shifted = ctx.enter_context(nc.semaphore("shifted"))
        exp_ready = ctx.enter_context(nc.semaphore("exp_ready"))
        chosen = ctx.enter_context(nc.semaphore("chosen"))
        counted = ctx.enter_context(nc.semaphore("counted"))
        dve_step = ctx.enter_context(nc.semaphore("dve_step"))

        def wide(a):
            return a.unsqueeze(2).to_broadcast(shape)

        with nc.Block() as block:
            @block.sync
            def _(sp):
                sp.dma_start(prefix[:, :], g["prefix_c"]).then_inc(consts_in, 16)
                sp.dma_start(rank[:, :], g["rank_c"]).then_inc(consts_in, 16)
                sp.wait_ge(consts_in, 32)

            @block.scalar
            def _(act):
                act.wait_ge(shifted, 1)
                nc.scalar.activation(probs[:, :, :], work[:, :, :], ACT.Exp).then_inc(exp_ready, 1)

            @block.tensor
            def _(pe):
                pe.wait_ge(chosen, 1)
                rhs = onehot16[:, :, :].rearrange("p t e -> p (t e)")
                nc.tensor.matmul(here_ps[:, :], prefix16[:, :], rhs, start=True, stop=True)
                nc.tensor.matmul(all_ps[:, :], all16[:, :], rhs, start=True, stop=True).then_inc(counted, 1)

            @block.vector
            def _(dve):
                steps = [0]

                def after(ins):
                    steps[0] += 1
                    ins.then_inc(dve_step, 1)
                    dve.wait_ge(dve_step, steps[0])

                V = nc.vector
                V.memset(all16[:, :], 1.0)
                V.memset(ones_row[:, :], 1.0)
                after(V.reduce_max(top[:, :], logits[:, :, :], AX.X))
                V.tensor_tensor(work[:, :, :], logits[:, :, :], wide(top[:, :]), ALU.subtract).then_inc(shifted, 1)
                dve.wait_ge(consts_in, 32)
                V.tensor_copy(prefix16[:, :], prefix[:, :])
                dve.wait_ge(exp_ready, 1)
                V.reduce_sum(total[:, :], probs[:, :, :], AX.X)
                after(V.reduce_max(top[:, :], probs[:, :, :], AX.X))
                after(V.reciprocal(first[:, :], total[:, :]))
                V.tensor_tensor(gate[:, :], top[:, :], first[:, :], ALU.mult)
                after(V.tensor_tensor(onehot[:, :, :], probs[:, :, :], wide(top[:, :]), ALU.is_ge))
                after(V.tensor_tensor(work[:, :, :], onehot[:, :, :], rank[:, :].unsqueeze(1).to_broadcast(shape), ALU.mult))
                after(V.reduce_max(first[:, :], work[:, :, :], AX.X))
                after(V.tensor_tensor(onehot[:, :, :], work[:, :, :], wide(first[:, :]), ALU.is_equal))
                V.tensor_copy(onehot16[:, :, :], onehot[:, :, :]).then_inc(chosen, 1)
                dve.wait_ge(counted, 1)
                after(V.tensor_copy(totals[:, :, :], all_ps[:, :].rearrange("p (t e) -> p t e", e=EXPERTS)))
                for e in range(EXPERTS):
                    last = V.tensor_tensor_scan(places[:, :, e], ones_row[:, :], totals[:, :, e], 0.0, ALU.mult, ALU.add)
                after(last)
                after(V.tensor_tensor(places[:, :, :], places[:, :, :], totals[:, :, :], ALU.subtract))
                after(V.tensor_tensor(places[:, :, :], here_ps[:, :].rearrange("p (t e) -> p t e", e=EXPERTS), places[:, :, :], ALU.add))
                after(V.tensor_scalar(work[:, :, :], places[:, :, :], CAPACITY + 0.5, None, ALU.is_lt))
                after(V.tensor_tensor(work[:, :, :], work[:, :, :], onehot[:, :, :], ALU.mult))
                after(V.reduce_sum(taken[:, :], work[:, :, :], AX.X))
                after(V.tensor_tensor(gate[:, :], gate[:, :], taken[:, :], ALU.mult))


def attend(nc, g):
    QB, CPB, STEPS, UNITS, HQ, DH, SCALE = (g[k] for k in ("QB", "CPB", "STEPS", "UNITS", "HQ", "DH", "SCALE"))
    ident = g["ident"]
    qk_dram, v_dram, a_dram = g["qk_dram"], g["v_dram"], g["a_dram"]
    TT = CH // P
    QT = CH // P
    KROWS = 3 * DH
    XROWS = KROWS + 2
    RP = 8
    GR = HQ * QT * (CPB // 2)
    EXPS = HQ * STEPS
    ON_PE = [3, 6, 9, 12, 14, 15]
    ON_POOL = [s for s in range(STEPS) if s not in ON_PE]
    ADDS = len(ON_POOL) - 1
    PLAN = [3, 2, 3, 2, 3, 2, 3, 2, 3, 2, 3, 2, 2, 0, 0, 0]
    assert sum(PLAN) == GR
    FINAL_STEP = 3
    INVERT_AT = 16
    DIVIDE_AT = 4
    TURN_STEP = 14
    FREE_GR, FREE_PV, FREE_EX = 2 * GR, STEPS, 2

    with ExitStack() as ctx:
        def sb(name, shape, dt):
            return ctx.enter_context(nc.sbuf_tensor(name, shape, dt))

        def pb(name, shape, dt):
            return ctx.enter_context(nc.psum_tensor(name, shape, dt))

        def sem(name):
            return ctx.enter_context(nc.semaphore(name))

        k_max = sb("k_max", [KROWS, HQ, CPB, CH], F16)
        k_exp = sb("k_exp", [XROWS, CPB, HQ, CH], F16)
        q_max = sb("q_max", [KROWS, 2, HQ, CH], F16)
        q_exp = sb("q_exp", [XROWS, 2, HQ, CH], F16)
        v_sb = sb("v_sb", [P, CPB, TT, P], F32)
        probs = sb("probs", [P, RP, HQ, CH], F32)
        acc = sb("acc", [P, 2, HQ, CH], F32)
        ones = sb("ones", [P, DH], F32)
        part = sb("part", [P, 2, GR], F32)
        row_max = sb("row_max", [P, GR // 2], F32)
        max_hi = sb("max_hi", [HQ * QT, 2, P], F16)
        max_lo = sb("max_lo", [HQ * QT, 2, P], F16)
        o_sb = sb("o_sb", [P, 2, CH], F32)
        d_sb = sb("d_sb", [P, 2, CH], F32)
        inv_sb = sb("inv_sb", [P, 2, CH], F32)
        a_sb = sb("a_sb", [P, 2, CH], F32)

        mx = [pb(f"mx{i}", [P, 2 * CH], F32) for i in range(2)]
        ex = [pb(f"ex{i}", [P, CH], F32) for i in range(2)]
        o_ps = pb("o_ps", [P, CH], F32)
        d_ps = pb("d_ps", [P, CH], F32)

        ones_set = sem("ones_set")
        kmax_in = [sem(f"kmax_in{h}") for h in range(HQ)]
        qmax_in = [sem(f"qmax_in{u}") for u in range(2)]
        qexp_in = [sem(f"qexp_in{u}") for u in range(2)]
        kv_in = [sem(f"kv_in{h}") for h in range(2)]
        rows_in = [sem(f"rows_in{u}") for u in range(2)]
        stored = [sem(f"stored{u}") for u in range(2)]
        mx_done = sem("mx_done")
        mx_read = sem("mx_read")
        row_ready = sem("row_ready")
        row_turned = sem("row_turned")
        hi_made = sem("hi_made")
        lo_made = sem("lo_made")
        ex_done = sem("ex_done")
        p_ready = sem("p_ready")
        pv_done = sem("pv_done")
        on_pe = sem("on_pe")
        on_pool = sem("on_pool")
        d_done = sem("d_done")
        o_read = sem("o_read")
        d_read = sem("d_read")
        inverted = sem("inverted")
        divided = sem("divided")

        with nc.Block() as block:
            @block.sync
            def _(sp):
                def halves(dst, src, order, s):
                    for r, half in enumerate(order):
                        sp.dma_start(dst[r * DH:(r + 1) * DH], src[half]).then_inc(s, 16)

                def load_kmax(qb, h):
                    src = qk_dram[qb, 1].rearrange("c l (h d) t -> l h d c t", h=HQ)
                    halves(k_max[:, h, :, :], [src[0, h], src[1, h]], (0, 0, 1), kmax_in[h])

                def load_qmax(qb, c):
                    src = qk_dram[qb, 0, c].rearrange("l (h d) t -> l d h t", h=HQ)
                    halves(q_max[:, c % 2, :, :], [src[0], src[1]], (0, 1, 0), qmax_in[c % 2])

                def load_qexp(qb, c):
                    src = qk_dram[qb, 0, c].rearrange("l (h d) t -> l d h t", h=HQ)
                    halves(q_exp[:, c % 2, :, :], [src[0], src[1]], (0, 1, 0), qexp_in[c % 2])

                def load_kv(qb, half):
                    for c in (2 * half, 2 * half + 1):
                        src = qk_dram[qb, 1, c].rearrange("l (h d) t -> l d h t", h=HQ)
                        halves(k_exp[:, c, :, :], [src[0], src[1]], (0, 0, 1), kv_in[half])
                        sp.dma_start(v_sb[:, c, :, :], v_dram[qb, c]).then_inc(kv_in[half], 16)

                def rows(qb, c):
                    v = qb * CPB + c
                    sp.wait_ge(lo_made, v + 1)
                    for r, src in ((KROWS, max_hi), (KROWS + 1, max_lo)):
                        dst = q_exp[r:r + 1, c % 2, :, :].rearrange("o h (j q) -> o (h j) q", q=P)
                        sp.dma_start(dst, src[:, c % 2, :]).then_inc(rows_in[c % 2], 16)

                def store(v, u):
                    sp.wait_ge(divided, v + 3)
                    sp.dma_start(a_dram[v], a_sb[:, u, :]).then_inc(stored[u], 16)

                def quad(qb, before, more):
                    for c in range(CPB):
                        v = qb * CPB + c
                        sp.wait_ge(o_read, v + 1)
                        load_qexp(qb, c)
                        if c + 1 < CPB or more:
                            sp.wait_ge(mx_read, v * GR + (FREE_GR))
                            if c + 1 < CPB:
                                load_qmax(qb, c + 1)
                            else:
                                load_qmax(qb + 1, 0)
                                for h in range(HQ):
                                    sp.wait_ge(mx_read, v * GR + (FREE_GR + (h + 1) * GR // HQ))
                                    load_kmax(qb + 1, h)
                        if c == 0:
                            sp.wait_ge(pv_done, v * STEPS + (FREE_PV - STEPS // 2))
                            load_kv(qb, 0)
                        rows(qb, c)
                        if c == 0:
                            sp.wait_ge(o_read, v + 2)
                            load_kv(qb, 1)
                        if c >= 2 or before:
                            store(v - 2, c % 2)

                for s in stored:
                    sp.sem_inc(s, 16)
                for h in range(HQ):
                    load_kmax(0, h)
                load_qmax(0, 0)
                quad(0, False, True)
                with sp.Fori(1, QB - 1) as qb:
                    quad(qb, True, True)
                quad(QB - 1, True, False)
                store(UNITS - 2, 0)
                store(UNITS - 1, 1)
                for s in stored:
                    sp.wait_ge(s, 16 * (1 + UNITS // 2))

            @block.vector
            def _(dve):
                dve.sem_inc(mx_read, FREE_GR)
                dve.sem_inc(inverted, 2)
                nc.vector.memset(ones[:, :], 1.0)
                nc.vector.memset(k_exp[KROWS:XROWS, :, :, :], MSCALE).then_inc(ones_set, 1)

                def invert(v, u):
                    dve.wait_ge(d_read, v + 2)
                    dve.wait_ge(divided, v + 1)
                    nc.vector.reciprocal(inv_sb[:, u, :], d_sb[:, u, :]).then_inc(inverted, 1)

                def maxima(v, u, before):
                    for n in range(GR):
                        if n == INVERT_AT and before:
                            invert(v - 2, u)
                        dve.wait_ge(mx_done, v * GR + (n + 1))
                        nc.vector.reduce_max(part[:, u, n:n + 1], mx[(u * (GR + 1) + n) % 2][:, :], AX.X).then_inc(mx_read, 1)
                    dve.wait_ge(mx_read, v * GR + (GR + FREE_GR))
                    nc.vector.tensor_tensor(row_max[:, :], part[:, u, 0:GR:2], part[:, u, 1:GR:2], ALU.max).then_inc(row_ready, 1)
                    turned = mx[(u * (GR + 1) + GR) % 2][0:HQ * QT, 0:P]
                    dve.wait_ge(row_turned, v + 1)
                    nc.vector.tensor_scalar(max_hi[:, u, :], turned, -1.0 / MSCALE, None, ALU.mult).then_inc(hi_made, 1)
                    dve.wait_ge(hi_made, v + 1)
                    nc.vector.scalar_tensor_tensor(out=max_lo[:, u, :], in0=turned, scalar=-1.0 / MSCALE, in1=max_hi[:, u, :],
                                                   op0=ALU.mult, op1=ALU.subtract).then_inc(lo_made, 1)

                maxima(0, 0, False)
                maxima(1, 1, False)
                with dve.Fori(1, UNITS // 2) as i:
                    maxima(i * 2, 0, True)
                    maxima(i * 2 + 1, 1, True)
                invert(UNITS - 2, 0)
                invert(UNITS - 1, 1)

            @block.gpsimd
            def _(pool):
                pool.sem_inc(on_pool, ADDS)
                pool.sem_inc(divided, 2)

                def divide(v, v2, u):
                    pool.wait_ge(o_read, v + 3)
                    pool.wait_ge(inverted, v + 3)
                    pool.wait_ge(stored[u], v2 * 16 + 16)
                    nc.gpsimd.tensor_tensor(a_sb[:, u, :], o_sb[:, u, :], inv_sb[:, u, :], ALU.mult).then_inc(divided, 1)

                def unit(v, v2, u, before):
                    pool.wait_ge(d_done, v + 1)
                    for n, s in enumerate(ON_POOL[1:]):
                        pool.wait_ge(p_ready, v * EXPS + (FREE_EX + HQ * (s + 1)))
                        a = probs[:, ON_POOL[0] + u * STEPS % RP, :, :] if n == 0 else acc[:, u, :, :]
                        if n:
                            pool.wait_ge(on_pool, v * ADDS + (ADDS + n))
                        nc.gpsimd.tensor_tensor(acc[:, u, :, :], a, probs[:, (u * STEPS + s) % RP, :, :], ALU.add).then_inc(on_pool, 1)
                        if n == DIVIDE_AT and before:
                            divide(v - 1, v2 - (1 - u), 1 - u)

                unit(0, 0, 0, False)
                unit(1, 0, 1, True)
                with pool.Fori(1, UNITS // 2) as i:
                    unit(i * 2, i, 0, True)
                    unit(i * 2 + 1, i, 1, True)
                divide(UNITS - 1, UNITS // 2 - 1, 1)

            @block.scalar
            def _(act):
                act.sem_inc(p_ready, FREE_EX)
                act.sem_inc(o_read, 2)
                act.sem_inc(d_read, 1)

                def read_o(v, u):
                    act.wait_ge(pv_done, v * STEPS + (FREE_PV + STEPS))
                    act.wait_ge(divided, v + 1)
                    nc.scalar.activation(o_sb[:, u, :], o_ps[:, :], ACT.Copy).then_inc(o_read, 1)

                def read_d(v, u):
                    act.wait_ge(d_done, v + 3)
                    act.wait_ge(inverted, v + 1)
                    nc.scalar.activation(d_sb[:, u, :], d_ps[:, :], ACT.Copy).then_inc(d_read, 1)

                def unit(v, u, before):
                    for s in range(STEPS):
                        for h in range(HQ):
                            n = HQ * s + h
                            act.wait_ge(ex_done, v * EXPS + (n + 1))
                            if h == 0:
                                old = s - RP
                                act.wait_ge(pv_done, v * STEPS + (FREE_PV + old + 1))
                                back, at = (1, old + STEPS) if old < 0 else (0, old)
                                if at in ON_PE:
                                    act.wait_ge(on_pe, v * len(ON_PE) + (len(ON_PE) * (1 - back) + ON_PE.index(at) + 1))
                                else:
                                    act.wait_ge(on_pool, v * ADDS + (ADDS * (1 - back) + max(ON_POOL.index(at), 1)))
                            nc.scalar.activation(probs[:, (u * STEPS + s) % RP, h, :], ex[n % 2][:, :], ACT.Exp, scale=SCALE).then_inc(p_ready, 1)
                        if s == 0 and before:
                            read_o(v - 1, 1 - u)
                        if s == FINAL_STEP and before:
                            read_d(v - 1, 1 - u)

                unit(0, 0, False)
                unit(1, 1, True)
                with act.Fori(1, UNITS // 2) as i:
                    unit(i * 2, 0, True)
                    unit(i * 2 + 1, 1, True)
                read_o(UNITS - 1, 1)
                read_d(UNITS - 1, 1)

            @block.tensor
            def _(pe):
                pe.sem_inc(pv_done, FREE_PV)
                pe.sem_inc(on_pe, len(ON_PE))
                pe.sem_inc(d_done, 2)
                pe.wait_ge(ones_set, 1)

                def max_group(v, v2, v4, u, n, first):
                    h, j, half = n // (2 * QT), n // 2 % QT, n % 2
                    if n == 0:
                        pe.wait_ge(qmax_in[u], (v2 + 1) * (3 * 16))
                    if n % (2 * QT) == 0:
                        pe.wait_ge(kmax_in[h], (v4 + 1) * (3 * 16))
                    if n != 1:
                        pe.wait_ge(mx_read, v * GR + (FREE_GR + n - 1 if n else FREE_GR))
                    elif not first:
                        pe.wait_ge(lo_made, v)
                    bank = mx[(u * (GR + 1) + n) % 2]
                    for k in range(2):
                        last = nc.tensor.matmul(bank[:, k * CH:(k + 1) * CH], q_max[:, u, h, j * P:(j + 1) * P], k_max[:, h, 2 * half + k, :],
                                                start=True, stop=True)
                    last.then_inc(mx_done, 1)

                def turn_rows(v, u):
                    pe.wait_ge(row_ready, v + 1)
                    bank = mx[(u * (GR + 1) + GR) % 2]
                    nc.tensor.transpose(bank[0:HQ * QT, 0:P], row_max[:, :], ident[:, :]).then_inc(row_turned, 1)

                def scores(v, u, s, h):
                    n = HQ * s + h
                    pe.wait_ge(p_ready, v * EXPS + (n + 1))
                    nc.tensor.matmul(ex[n % 2][:, :], k_exp[:, s // TT, h, s % TT * P:(s % TT + 1) * P], q_exp[:, u, h, :],
                                     start=True, stop=True).then_inc(ex_done, 1)

                def sums(v, u, s):
                    pe.wait_ge(p_ready, v * EXPS + (FREE_EX + HQ * (s + 1)))
                    if s == 0:
                        pe.wait_ge(o_read, v + 2)
                    for h in range(HQ):
                        last = nc.tensor.matmul(o_ps[h * DH:(h + 1) * DH, :], v_sb[:, s // TT, s % TT, h * DH:(h + 1) * DH],
                                                probs[:, (u * STEPS + s) % RP, h, :], start=(s == 0), stop=(s == STEPS - 1))
                    last.then_inc(pv_done, 1)
                    if s in ON_PE:
                        if s == ON_PE[0]:
                            pe.wait_ge(d_read, v + 1)
                        for h in range(HQ):
                            last = nc.tensor.matmul(d_ps[h * DH:(h + 1) * DH, :], ones[:, :], probs[:, (u * STEPS + s) % RP, h, :],
                                                    start=(s == ON_PE[0]), stop=False)
                        last.then_inc(on_pe, 1)

                def close(v, u):
                    pe.wait_ge(on_pool, v * ADDS + 2 * ADDS)
                    for h in range(HQ):
                        last = nc.tensor.matmul(d_ps[h * DH:(h + 1) * DH, :], ones[:, :], acc[:, u, h, :], start=False, stop=True)
                    last.then_inc(d_done, 1)

                def unit(v, v2, v4, w2, w4, u, before, after):
                    n = 0
                    for s in range(STEPS):
                        if s == 0:
                            pe.wait_ge(qexp_in[u], (v2 + 1) * (3 * 16))
                            pe.wait_ge(rows_in[u], (v2 + 1) * (2 * 16))
                        if s % (STEPS // 2) == 0:
                            pe.wait_ge(kv_in[s // (STEPS // 2)], (v4 + 1) * (8 * 16))
                        scores(v, u, s, 0)
                        scores(v, u, s, 1)
                        groups = PLAN[s] if after else 0
                        if groups:
                            max_group(v + 1, w2, w4, 1 - u, n, False)
                            n += 1
                        if s:
                            sums(v, u, s - 1)
                        elif before:
                            sums(v - 1, 1 - u, STEPS - 1)
                        if s == FINAL_STEP and before:
                            close(v - 1, 1 - u)
                        scores(v, u, s, 2)
                        scores(v, u, s, 3)
                        for _ in range(groups - 1):
                            max_group(v + 1, w2, w4, 1 - u, n, False)
                            n += 1
                        if s == TURN_STEP and after:
                            turn_rows(v + 1, 1 - u)

                def pair(i, before=True, after=True):
                    v = i * 2
                    unit(v, i, v // CPB, i, (v + 1) // CPB, 0, before, True)
                    unit(v + 1, i, (v + 1) // CPB, i + 1, (v + 2) // CPB, 1, True, after)

                for n in range(GR):
                    max_group(0, 0, 0, 0, n, True)
                turn_rows(0, 0)
                pair(0, before=False)
                with pe.Fori(1, UNITS // 2 - 1) as i:
                    pair(i)
                pair(UNITS // 2 - 1, after=False)
                sums(UNITS - 1, 1, STEPS - 1)
                close(UNITS - 1, 1)


def finish_rows(nc, g):
    B, CPB, QUADS, D, NCH = (g[k] for k in ("B", "CPB", "QUADS", "D", "NCH"))
    TT = CH // P
    RING = 4
    w_out_sb, b_out_sb, gate = g["w_out_sb"], g["b_out_sb"], g["gate"]
    with ExitStack() as ctx:
        def sb(name, shape, dt):
            return ctx.enter_context(nc.sbuf_tensor(name, shape, dt))

        def sem(name):
            return ctx.enter_context(nc.semaphore(name))

        a_in = sb("a_in", [P, 2, QUADS, CH], F32)
        x_in = sb("x_in", [P, 2, TT, D], F32)
        y_in = sb("y_in", [P, 2, TT, D], F32)
        g_now = sb("g_now", [P, 2, TT], F32)
        o_out = sb("o_out", [P, 2, TT, D], F32)
        prod = [ctx.enter_context(nc.psum_tensor(f"prod{i}", [P, D], F32)) for i in range(RING)]
        loaded = [sem(f"loaded{u}") for u in range(2)]
        out_stored = [sem(f"out_stored{u}") for u in range(2)]
        gates = sem("gates")
        biased = sem("biased")
        multiplied = sem("multiplied")
        gated = sem("gated")
        summed = sem("summed")

        with nc.Block() as block:
            @block.sync
            def _(sp):
                for s in out_stored:
                    sp.sem_inc(s, 16)
                a_view = g["a_dram"].rearrange("(b q c) p t -> b c p q t", b=B, q=QUADS)
                rows = [t.rearrange("(b c t p) d -> b c p t d", b=B, c=CPB, t=TT) for t in (g["x_rows"], g["y_dram"], g["out_rows"])]
                with sp.Fori(0, B) as b:
                    with sp.Fori(0, CPB // 2) as ci:
                        for u in range(2):
                            c = b * CPB + ci * 2 + u
                            sp.wait_ge(summed, c + 1)
                            ch = ci * 2 + u
                            sp.dma_start(a_in[:, u, :, :], a_view[b, ch]).then_inc(loaded[u], 16)
                            sp.dma_start(y_in[:, u, :, :], rows[1][b, ch]).then_inc(loaded[u], 16)
                            sp.dma_start(x_in[:, u, :, :], rows[0][b, ch]).then_inc(loaded[u], 16)

            @block.scalar
            def _(act):
                view = g["out_rows"].rearrange("(i u t p) d -> i u p t d", u=2, t=TT, p=P)
                with act.Fori(0, NCH // 2) as i:
                    for u in range(2):
                        act.wait_ge(summed, i * 2 + (u + 3))
                        act.dma_start(view[i, u], o_out[:, u, :, :]).then_inc(out_stored[u], 16)
                for s in out_stored:
                    act.wait_ge(s, 16 * (1 + NCH // 2))

            @block.gpsimd
            def _(pool):
                with pool.Fori(0, NCH // 2) as i:
                    for u in range(2):
                        pool.wait_ge(loaded[u], i * 48 + 48)
                        nc.gpsimd.tensor_tensor(x_in[:, u, :, :], x_in[:, u, :, :],
                                                b_out_sb[:, :].unsqueeze(1).to_broadcast([P, TT, D]), ALU.add).then_inc(biased, 1)

            @block.tensor
            def _(pe):
                with pe.Fori(0, NCH // 2) as i:
                    for u in range(2):
                        pe.wait_ge(loaded[u], i * 48 + 48)
                        for t in range(TT):
                            pe.wait_ge(gated, (i * 2 + u) * TT + (t + 1))
                            for q in range(QUADS):
                                last = nc.tensor.matmul(prod[t][:, :], a_in[:, u, q, t * P:(t + 1) * P], w_out_sb[:, q, :],
                                                        start=(q == 0), stop=(q == QUADS - 1))
                            last.then_inc(multiplied, 1)

            @block.vector
            def _(dve):
                dve.sem_inc(gated, RING)
                dve.sem_inc(summed, 2)
                with dve.Fori(0, NCH // 2) as i:
                    for u in range(2):
                        c = i * 2 + u
                        nc.vector.tensor_copy(g_now[:, u, :], gate[:, bass.ds(c * TT, TT)]).then_inc(gates, 1)
                        dve.wait_ge(loaded[u], i * 48 + 48)
                        dve.wait_ge(gates, c + 1)
                        dve.wait_ge(out_stored[u], i * 16 + 16)
                        for t in range(TT):
                            dve.wait_ge(multiplied, c * TT + (t + 1))
                            nc.vector.scalar_tensor_tensor(out=o_out[:, u, t, :], in0=y_in[:, u, t, :], scalar=g_now[:, u, t:t + 1],
                                                           in1=prod[t][:, :], op0=ALU.mult, op1=ALU.add).then_inc(gated, 1)
                        dve.wait_ge(biased, c + 1)
                        dve.wait_ge(gated, c * TT + (TT + RING))
                        nc.vector.tensor_tensor(o_out[:, u, :, :], o_out[:, u, :, :], x_in[:, u, :, :], ALU.add).then_inc(summed, 1)


_INS = ["L0_attn_x", "L0_attn_w_qkv", "L0_attn_w_out", "L0_attn_b_out", "L0_attn_mask_logits",
        "L0_ffn_w_gate", "L0_ffn_w_expert", "L0_ffn_b_expert"]


def _constants():
    import numpy as np
    dh, heads = 32, 4
    n = np.arange(dh)
    rows = [np.sqrt((1.0 if f in (0, dh // 2) else 2.0) / dh) * np.cos(2 * np.pi * f * n / dh) for f in range(dh // 2 + 1)]
    rows += [np.sqrt(2.0 / dh) * np.sin(2 * np.pi * f * n / dh) for f in range(1, dh // 2)]
    basis = np.kron(np.eye(heads), np.stack(rows)).astype(np.float32)
    prefix = np.triu(np.ones((P, P))).astype(np.float32)
    rank = np.tile(np.arange(EXPERTS, 0, -1), (P, 1)).astype(np.float32)
    return {"ident": np.eye(P, dtype=np.float32), "basis": basis, "prefix": prefix, "rank": rank}


def kernel(**inputs):
    import numpy as np
    import concourse.bacc as bacc
    from concourse.bass_utils import run_bass_kernel_spmd

    nc = bacc.Bacc("TRN2", target_bir_lowering=False, num_devices=1)
    arrays, args = {}, []
    for name, a in [(n, inputs[n]) for n in _INS] + list(_constants().items()):
        a = np.ascontiguousarray(a)
        arrays[f"in_{name}"] = a
        args.append(nc.dram_tensor(f"in_{name}", a.shape, mybir.dt.from_np(a.dtype), kind="ExternalInput").ap())
    out = nc.dram_tensor("out_0", inputs["L0_attn_x"].shape, F32, kind="ExternalOutput").ap()
    attention_and_experts_kernel(nc, *args, out)
    r = run_bass_kernel_spmd(nc, [arrays], core_ids=[0])
    return r.results[0]["out_0"]
```

```python
from contextlib import ExitStack

import concourse.bass as bass
from concourse import mybir

F32 = mybir.dt.float32
F16 = mybir.dt.float16
BF16 = mybir.dt.bfloat16
ALU = mybir.AluOpType
ACT = mybir.ActivationFunctionType
AX = mybir.AxisListType

P = 128
CH = 512
EXPERTS = 8
CAPACITY = 100
EPS = 1e-5
XSCALE = 2.0 ** 10
WTOP = 2.0 ** 14
MSCALE = 256.0


def attention_and_experts_kernel(nc, x, w_qkv, w_out, b_out, mask_logits, w_gate, w_expert, b_expert,
                                 ident_c, basis_c, prefix_c, rank_c, out):
    B, S, D = x.shape
    DH = 32
    NF = mask_logits.shape[0]
    HQ = P // DH
    QUADS = D // P
    KB = D // P
    TT = CH // P
    CPB = S // CH
    NCH = B * CPB
    QB = B * QUADS
    NT = B * S // P
    STEPS = S // P
    UNITS = QB * CPB
    SCALE = float(DH) ** -0.5
    assert D == CH and DH == 32 and NF == DH // 2 + 1

    x_rows = x.rearrange("b s d -> (b s) d")
    out_rows = out.rearrange("b s d -> (b s) d")
    qk_dram = nc.dram_tensor("qk_scratch", (QB, 2, CPB, 2, P, CH), F16).ap()
    v_dram = nc.dram_tensor("v_scratch", (QB, CPB, P, TT, P), F32).ap()
    y_dram = nc.dram_tensor("y_scratch", (B * S, D), F32).ap()
    a_dram = nc.dram_tensor("attn_scratch", (UNITS, P, CH), F32).ap()

    with ExitStack() as whole:
        def keep(name, shape, dt):
            return whole.enter_context(nc.sbuf_tensor(name, shape, dt))

        ident = keep("ident", [P, P], F32)
        w_out_sb = keep("w_out_sb", [P, QUADS, D], F32)
        b_out_sb = keep("b_out_sb", [P, D], F32)
        logits = keep("logits", [P, NT, EXPERTS], F32)
        gate = keep("gate", [P, NT], F32)

        project(nc, locals())
        route(nc, locals())
        attend(nc, locals())
        finish_rows(nc, locals())


def project(nc, g):
    D, DH, NF, HQ, QUADS, KB, TT, CPB, NCH = (g[k] for k in ("D", "DH", "NF", "HQ", "QUADS", "KB", "TT", "CPB", "NCH"))
    B = g["B"]
    ident, logits = g["ident"], g["logits"]
    MB = 2 * D // P
    QK_RING, V_RING, Y_RING, MM_RING = 4, 2, 2, 4
    PRODUCTS = [(0, 0), (0, 1), (1, 0)]
    GROUPS = MB + 2 * TT

    with ExitStack() as ctx:
        def sb(name, shape, dt):
            return ctx.enter_context(nc.sbuf_tensor(name, shape, dt))

        def pb(name, shape, dt):
            return ctx.enter_context(nc.psum_tensor(name, shape, dt))

        def sem(name):
            return ctx.enter_context(nc.semaphore(name))

        w_qkv_sb = sb("w_qkv_sb", [P, KB, 3 * D], F32)
        w_filt = sb("w_filt", [P, KB, 2 * D], F32)
        w_exp_sb = sb("w_exp_sb", [P, KB, D], F32)
        qk_w = sb("qk_w", [P, 2, KB, 2 * D], F16)
        v_w = sb("v_w", [P, 2, KB, D], F16)
        exp_w = sb("exp_w", [P, 2, KB, D], F16)
        gate_w = sb("gate_w", [P, 2, KB, DH], F16)
        w_max = sb("w_max", [P, 5], F32)
        w_top = sb("w_top", [P, 5], F32)
        power = sb("power", [P, 5], F32)
        w_scale = sb("w_scale", [P, 5], F32)
        w_inv = sb("w_inv", [P, 5], F32)
        balance = sb("balance", [P, 4], F32)
        w_gate_sb = sb("w_gate_sb", [P, KB, DH], F32)
        b_exp_sb = sb("b_exp_sb", [P, D], F32)
        basis = sb("basis", [P, P], F32)
        basis_m = sb("basis_m", [P, P], F32)
        filt = sb("filt", [P, P], F32)
        mask = sb("mask", [P, 3], F32)
        eps = sb("eps", [P, 1], F32)
        wt = sb("wt", [P, 2, D], F32)
        xs = sb("xs", [P, 2, TT, D], F32)
        xt = sb("xt", [P, 2, 2, KB, CH], F16)
        stats = sb("stats", [P, TT, 6], F32)
        mean_var = sb("mean_var", [P, TT, 2], F32)
        std = sb("std", [P, TT], F32)
        rstd = sb("rstd", [P, TT], F32)
        qk_out = sb("qk_out", [P, QK_RING, 2, CH], F16)
        v_out = sb("v_out", [P, V_RING, D], F32)
        y_out = sb("y_out", [P, Y_RING, D], F32)
        lg_sb = sb("lg_sb", [P, CH], F32)

        mm = [pb(f"mm{i}", [P, CH], F32) for i in range(MM_RING)]
        xt_ps = [pb(f"xt_ps{i}", [P, CH], F32) for i in range(2)]
        lg_ps = pb("lg_ps", [P, CH], F32)
        lt_ps = pb("lt_ps", [P, CH], F32)

        weights_in = sem("weights_in")
        zeroed = sem("zeroed")
        mask_exp = sem("mask_exp")
        mask_step = sem("mask_step")
        basis_ready = sem("basis_ready")
        filt_made = sem("filt_made")
        filt_ready = sem("filt_ready")
        wt_made = sem("wt_made")
        wt_ready = sem("wt_ready")
        wf_made = sem("wf_made")
        wf_ready = sem("wf_ready")
        w_maxed = sem("w_maxed")
        w_topped = sem("w_topped")
        ratio_ready = sem("ratio_ready")
        root_ready = sem("root_ready")
        dve_step = sem("dve_step")

        with nc.Block() as block:
            @block.sync
            def _(sp):
                n = 0
                view = mask[:, 0:1]
                ml = g["mask_logits"].rearrange("(f o) -> f o", o=1)
                loads = [
                    (w_qkv_sb[:, :, :], g["w_qkv"].rearrange("(j p) n -> p j n", p=P)),
                    (ident[:, :], g["ident_c"]), (basis[:, :], g["basis_c"]),
                    (w_exp_sb[:, :, :], g["w_expert"].rearrange("(j p) n -> p j n", p=P)),
                    (b_exp_sb[:, :], g["b_expert"].partition_broadcast(P)),
                    (g["b_out_sb"][:, :], g["b_out"].partition_broadcast(P)),
                    (g["w_out_sb"][:, :, :], g["w_out"].rearrange("(j p) n -> p j n", p=P)),
                ]
                for h in range(HQ):
                    loads.append((view[h * DH:h * DH + NF, :], ml))
                    loads.append((view[h * DH + NF:(h + 1) * DH, :], ml[1:NF - 1, :]))
                for dst, src in loads:
                    sp.dma_start(dst, src).then_inc(weights_in, 16)
                    n += 16
                sp.wait_ge(zeroed, 1)
                sp.dma_start(w_gate_sb[:, :, 0:EXPERTS], g["w_gate"].rearrange("(j p) n -> p j n", p=P)).then_inc(weights_in, 16)
                sp.wait_ge(weights_in, n + 16)

            n_loads = 7 + 2 * HQ + 1

            @block.scalar
            def _(act):
                act.wait_ge(weights_in, 16 * n_loads)
                nc.scalar.activation(mask[:, 1:2], mask[:, 0:1], ACT.Exp, scale=-1.0).then_inc(mask_exp, 1)
                for m in range(MB):
                    act.wait_ge(wf_made, m + 1)
                    nc.scalar.activation(w_filt[:, :, m * P:(m + 1) * P],
                                         mm[m % 2][:, :].rearrange("p (j n) -> p j n", j=KB), ACT.Copy).then_inc(wf_ready, 1)
                act.wait_ge(ratio_ready, 1)
                nc.scalar.activation(balance[:, 1:2], balance[:, 0:1], ACT.Sqrt).then_inc(root_ready, 1)

            @block.gpsimd
            def _(pool):
                for n, (a, b) in enumerate(((0, 3), (3, 5))):
                    pool.wait_ge(w_maxed, n + 1)
                    nc.gpsimd.partition_all_reduce(w_top[:, a:b], w_max[:, a:b], P, bass.bass_isa.ReduceOp.max).then_inc(w_topped, 1)

            @block.vector
            def _(dve):
                nc.vector.memset(w_gate_sb[:, :, :], 0.0).then_inc(zeroed, 1)
                nc.vector.memset(eps[:, :], EPS / XSCALE ** 2)
                steps = [0]

                def after(ins):
                    steps[0] += 1
                    ins.then_inc(dve_step, 1)
                    dve.wait_ge(dve_step, steps[0])

                def largest(n, w):
                    return nc.vector.tensor_reduce(out=w_max[:, n:n + 1], in_=w, op=ALU.max, axis=AX.XY, apply_absolute_value=True)

                def scales(a, b):
                    after(nc.vector.tensor_scalar_max(power[:, a:b], w_top[:, a:b], 2.0 ** -100))
                    bits = power[:, a:b].bitcast(mybir.dt.int32)
                    after(nc.vector.tensor_scalar(bits, bits, 0x7F800000, None, ALU.bitwise_and))
                    after(nc.vector.reciprocal(w_scale[:, a:b], power[:, a:b]))
                    nc.vector.tensor_scalar(w_inv[:, a:b], power[:, a:b], 1.0 / (WTOP * XSCALE), None, ALU.mult)
                    after(nc.vector.tensor_scalar(w_scale[:, a:b], w_scale[:, a:b], WTOP, None, ALU.mult))

                def split(halves, w, n):
                    after(nc.vector.tensor_scalar(halves[:, 0], w, w_scale[:, n:n + 1], None, ALU.mult))
                    nc.vector.scalar_tensor_tensor(out=halves[:, 1], in0=w, scalar=w_scale[:, n:n + 1], in1=halves[:, 0],
                                                   op0=ALU.mult, op1=ALU.subtract)

                dve.wait_ge(weights_in, 16 * n_loads)
                dve.wait_ge(mask_exp, 1)
                nc.vector.tensor_scalar_add(mask[:, 2:3], mask[:, 1:2], 1.0).then_inc(mask_step, 1)
                dve.wait_ge(mask_step, 1)
                nc.vector.reciprocal(mask[:, 1:2], mask[:, 2:3]).then_inc(mask_step, 1)
                dve.wait_ge(mask_step, 2)
                nc.vector.tensor_scalar(basis_m[:, :], basis[:, :], mask[:, 1:2], None, ALU.mult).then_inc(basis_ready, 1)
                largest(0, w_qkv_sb[:, :, 2 * D:3 * D])
                largest(1, w_exp_sb[:, :, :])
                largest(2, w_gate_sb[:, :, :]).then_inc(w_maxed, 1)
                dve.wait_ge(filt_made, 1)
                nc.vector.tensor_copy(filt[:, :], lg_ps[:, 0:P]).then_inc(filt_ready, 1)
                for m in range(MB):
                    dve.wait_ge(wt_made, m + 1)
                    if m >= 2:
                        dve.wait_ge(wf_made, m - 1)
                    nc.vector.tensor_copy(wt[:, m % 2, :], xt_ps[m % 2][:, :]).then_inc(wt_ready, 1)
                dve.wait_ge(wf_ready, MB)
                for n in range(2):
                    last = largest(3 + n, w_filt[:, :, n * D:(n + 1) * D])
                last.then_inc(w_maxed, 1)
                dve.wait_ge(w_topped, 1)
                scales(0, 3)
                split(v_w, w_qkv_sb[:, :, 2 * D:3 * D], 0)
                split(exp_w, w_exp_sb[:, :, :], 1)
                split(gate_w, w_gate_sb[:, :, :], 2)
                dve.wait_ge(w_topped, 2)
                scales(3, 5)
                for n in range(2):
                    split(qk_w[:, :, :, n * D:(n + 1) * D], w_filt[:, :, n * D:(n + 1) * D], 3 + n)
                after(nc.vector.reciprocal(balance[:, 2:3], power[:, 3:4]))
                after(nc.vector.tensor_tensor(balance[:, 3:4], power[:, 4:5], balance[:, 2:3], ALU.mult))
                nc.vector.tensor_scalar(balance[:, 0:1], balance[:, 3:4], 2.0 ** -100, 2.0 ** 100, ALU.max, ALU.min).then_inc(ratio_ready, 1)
                dve.wait_ge(root_ready, 1)
                bits = balance[:, 1:2].bitcast(mybir.dt.int32)
                after(nc.vector.tensor_scalar(bits, bits, 0x7F800000, None, ALU.bitwise_and))
                after(nc.vector.reciprocal(balance[:, 2:3], balance[:, 1:2]))
                nc.vector.tensor_tensor(w_inv[:, 3:5], w_inv[:, 3:5], balance[:, 1:3], ALU.mult)

            @block.tensor
            def _(pe):
                pe.wait_ge(weights_in, 16 * n_loads)
                pe.wait_ge(basis_ready, 1)
                nc.tensor.matmul(lg_ps[:, 0:P], basis_m[:, :], basis[:, :], start=True, stop=True).then_inc(filt_made, 1)

                def turn(m):
                    if m >= 2:
                        pe.wait_ge(wt_ready, m - 1)
                    for j in range(KB):
                        last = nc.tensor.transpose(xt_ps[m % 2][:, j * P:(j + 1) * P], w_qkv_sb[:, j, m * P:(m + 1) * P], ident[:, :])
                    last.then_inc(wt_made, 1)

                turn(0)
                pe.wait_ge(filt_ready, 1)
                for m in range(MB):
                    if m + 1 < MB:
                        turn(m + 1)
                    pe.wait_ge(wt_ready, m + 1)
                    if m >= 2:
                        pe.wait_ge(wf_ready, m - 1)
                    for j in range(KB):
                        last = nc.tensor.matmul(mm[m % 2][:, j * P:(j + 1) * P], wt[:, m % 2, j * P:(j + 1) * P], filt[:, :],
                                                start=True, stop=True, skip_group_check=True)
                    last.then_inc(wf_made, 1)

        x_in = [sem(f"x_in{u}") for u in range(2)]
        x_turned = sem("x_turned")
        varied = sem("varied")
        stats_seen = sem("stats_seen")
        aggregated = sem("aggregated")
        std_ready = sem("std_ready")
        rstd_ready = sem("rstd_ready")
        xn_ready = sem("xn_ready")
        xt_made = sem("xt_made")
        xt_high = sem("xt_high")
        xt_ready = sem("xt_ready")
        lg_made = sem("lg_made")
        lg_ready = sem("lg_ready")
        lt_made = sem("lt_made")
        lt_summed = sem("lt_summed")
        mm_done = sem("mm_done")
        hi_ready = sem("hi_ready")
        lo_ready = sem("lo_ready")
        v_ready = sem("v_ready")
        y_ready = sem("y_ready")
        qk_stored = [sem(f"qk_stored{i}") for i in range(QK_RING)]
        v_stored = [sem(f"v_stored{i}") for i in range(V_RING)]
        y_stored = [sem(f"y_stored{i}") for i in range(Y_RING)]
        PAIRS = NCH // 2

        with nc.Block() as block:
            @block.gpsimd
            def _(pool):
                with pool.Fori(0, PAIRS) as i:
                    for u in range(2):
                        pool.wait_ge(x_turned, i * 2 + (u + 1))
                        nc.gpsimd.dma_start(xs[:, u, :, :],
                                            g["x_rows"].rearrange("(i u t p) d -> i u p t d", u=2, t=TT, p=P)[i, u]).then_inc(x_in[u], 16)

            @block.sync
            def _(sp):
                for s in (*qk_stored, *v_stored, *y_stored):
                    sp.sem_inc(s, 16)
                y_view = g["y_dram"].rearrange("(b c t p) d -> b c t p d", b=B, c=CPB, t=TT)
                with sp.Fori(0, B) as b:
                    with sp.Fori(0, CPB // 2) as ci:
                        for u in range(2):
                            c = b * CPB + ci * 2 + u
                            ch = ci * 2 + u
                            for m in range(MB):
                                sp.wait_ge(lo_ready, c * MB + (m + 1))
                                dst = g["qk_dram"].rearrange("(b q) k c l p t -> b q k c p l t", b=B)[b, m % QUADS, m // QUADS, ch]
                                sp.dma_start(dst, qk_out[:, m % QK_RING, :, :]).then_inc(qk_stored[m % QK_RING], 16)
                            for t in range(TT):
                                sp.wait_ge(v_ready, c * TT + (t + 1))
                                dst = g["v_dram"].rearrange("(b q) c p t n -> b c t p q n", b=B)[b, ch, t]
                                sp.dma_start(dst, v_out[:, t % V_RING, :].rearrange("p (q n) -> p q n", q=QUADS)).then_inc(v_stored[t % V_RING], 16)
                            for t in range(TT):
                                sp.wait_ge(y_ready, c * TT + (t + 1 + TT))
                                sp.dma_start(y_view[b, ch, t], y_out[:, t % Y_RING, :]).then_inc(y_stored[t % Y_RING], 16)
                for s in qk_stored:
                    sp.wait_ge(s, 16 * (1 + NCH * MB // QK_RING))
                for s in v_stored:
                    sp.wait_ge(s, 16 * (1 + NCH * TT // V_RING))
                for s in y_stored:
                    sp.wait_ge(s, 16 * (1 + NCH * TT // Y_RING))

            @block.scalar
            def _(act):
                act.sem_inc(lg_ready, 1)

                def deviation(c):
                    act.wait_ge(aggregated, c + 1)
                    nc.scalar.activation(std[:, :], mean_var[:, :, 1], ACT.Sqrt, bias=eps[:, 0:1], scale=XSCALE ** -2).then_inc(std_ready, 1)

                def turned(c, u):
                    for j in range(KB):
                        act.wait_ge(xt_made, c * KB + (j + 1))
                        nc.scalar.activation(xt[:, u, 0, j, :], xt_ps[j % 2][:, :], ACT.Copy).then_inc(xt_high, 1)

                def chunk(c, u, more):
                    act.wait_ge(lg_made, c + 1)
                    act.wait_ge(lt_made, c + 1)
                    nc.scalar.activation(lg_sb[:, :], lg_ps[:, :], ACT.Copy, scale=w_inv[:, 2:3]).then_inc(lg_ready, 1)
                    for m in range(MB):
                        act.wait_ge(mm_done, c * GROUPS + (m + 1))
                        act.wait_ge(qk_stored[m % QK_RING], (c * (MB // QK_RING) + (m // QK_RING + 1)) * 16)
                        nc.scalar.activation(qk_out[:, m % QK_RING, 0, :], mm[m % MM_RING][:, :], ACT.Copy,
                                             scale=w_inv[:, 3 + m // QUADS:4 + m // QUADS]).then_inc(hi_ready, 1)
                        if m == 5 and more:
                            deviation(c + 1)
                    if more:
                        turned(c + 1, 1 - u)
                    for t in range(TT):
                        act.wait_ge(mm_done, c * GROUPS + (MB + t + 1))
                        act.wait_ge(v_stored[t % V_RING], (c * (TT // V_RING) + (t // V_RING + 1)) * 16)
                        nc.scalar.activation(v_out[:, t % V_RING, :], mm[(MB + t) % MM_RING][:, :], ACT.Copy, scale=w_inv[:, 0:1]).then_inc(v_ready, 1)

                deviation(0)
                turned(0, 0)
                with act.Fori(0, PAIRS - 1) as i:
                    chunk(i * 2, 0, True)
                    chunk(i * 2 + 1, 1, True)
                chunk(NCH - 2, 0, True)
                chunk(NCH - 1, 1, False)

            @block.vector
            def _(dve):
                dve.sem_inc(y_ready, TT)
                dve.sem_inc(lt_summed, 1)
                dve.sem_inc(xt_ready, 2)

                def low_halves(c, u):
                    for j in range(KB):
                        dve.wait_ge(xt_high, c * KB + (j + 1))
                        nc.vector.tensor_tensor(xt[:, u, 1, j, :], xt_ps[j % 2][:, :], xt[:, u, 0, j, :], ALU.subtract).then_inc(xt_ready, 1)

                def moments(c, c2, u):
                    dve.wait_ge(x_in[u], (c2 + 1) * 16)
                    for t in range(TT):
                        last = nc.vector.bn_stats(stats[:, t, :], xs[:, u, t, :])
                    last.then_inc(varied, 1)
                    dve.wait_ge(varied, c + 1)
                    dve.sem_inc(stats_seen, 1)
                    for t in range(TT):
                        last = nc.vector.bn_aggr(mean_var[:, t, :], stats[:, t, :])
                    last.then_inc(aggregated, 1)

                def normalise(c, u):
                    dve.wait_ge(std_ready, c + 1)
                    nc.vector.reciprocal(rstd[:, :], std[:, :]).then_inc(rstd_ready, 1)
                    dve.wait_ge(rstd_ready, c + 1)
                    for t in range(TT):
                        last = nc.vector.tensor_scalar(xs[:, u, t, :], xs[:, u, t, :], mean_var[:, t, 0:1], rstd[:, t:t + 1],
                                                       ALU.subtract, ALU.mult)
                    last.then_inc(xn_ready, 1)

                def chunk(c, c2, u, more):
                    for m in range(MB):
                        dve.wait_ge(hi_ready, c * MB + (m + 1))
                        nc.vector.scalar_tensor_tensor(out=qk_out[:, m % QK_RING, 1, :], in0=mm[m % MM_RING][:, :],
                                                       scalar=w_inv[:, 3 + m // QUADS:4 + m // QUADS], in1=qk_out[:, m % QK_RING, 0, :],
                                                       op0=ALU.mult, op1=ALU.subtract).then_inc(lo_ready, 1)
                        if m == 3 and more:
                            moments(c + 1, c2 + u, 1 - u)
                        if m == 5 and more:
                            normalise(c + 1, 1 - u)
                    if more:
                        low_halves(c + 1, 1 - u)
                    dve.wait_ge(lt_made, c + 2)
                    nc.vector.tensor_reduce(out=logits[:, bass.ds(c * TT, TT), :],
                                            in_=lt_ps[:, :].rearrange("p (t j e) -> p t e j", t=TT, j=KB)[:, :, 0:EXPERTS, :],
                                            op=ALU.add, axis=AX.X).then_inc(lt_summed, 1)
                    for t in range(TT):
                        dve.wait_ge(mm_done, c * GROUPS + (MB + TT + t + 1))
                        dve.wait_ge(y_stored[t % Y_RING], (c * (TT // Y_RING) + (t // Y_RING + 1)) * 16)
                        nc.vector.scalar_tensor_tensor(out=y_out[:, t % Y_RING, :], in0=mm[(MB + TT + t) % MM_RING][:, :],
                                                       scalar=w_inv[:, 1:2], in1=b_exp_sb[:, :],
                                                       op0=ALU.mult, op1=ALU.add).then_inc(y_ready, 1)

                moments(0, 0, 0)
                normalise(0, 0)
                low_halves(0, 0)
                with dve.Fori(0, PAIRS - 1) as i:
                    chunk(i * 2, i, 0, True)
                    chunk(i * 2 + 1, i, 1, True)
                chunk(NCH - 2, PAIRS - 1, 0, True)
                chunk(NCH - 1, PAIRS - 1, 1, False)

            @block.tensor
            def _(pe):
                pe.sem_inc(x_turned, 2)
                pe.sem_inc(lt_made, 1)

                def turn(c, u):
                    pe.wait_ge(xn_ready, c + 1)
                    for j in range(KB):
                        pe.wait_ge(xt_ready, c * KB + (j + 1))
                        for t in range(TT):
                            last = nc.tensor.transpose(xt_ps[j % 2][:, t * P:(t + 1) * P], xs[:, u, t, j * P:(j + 1) * P], ident[:, :])
                        last.then_inc(xt_made, 1)
                    pe.wait_ge(xt_ready, c * KB + (KB + 2))
                    pe.sem_inc(x_turned, 1)

                def group(c, n, lhs, rhs):
                    if n < TT:
                        pe.wait_ge(y_ready, c * TT + (n + 1))
                    elif n < MB + TT:
                        pe.wait_ge(lo_ready, c * MB + (n - MM_RING + 1))
                    else:
                        pe.wait_ge(v_ready, c * TT + (n - MB - TT + 1))
                    for j in range(KB):
                        for k, (a, b) in enumerate(PRODUCTS):
                            last = nc.tensor.matmul(mm[n % MM_RING][:, :], lhs(a, j), rhs(b, j), start=(j == k == 0),
                                                    stop=(j == KB - 1 and k == len(PRODUCTS) - 1))
                    last.then_inc(mm_done, 1)

                def chunk(c, u, more):
                    pe.wait_ge(xt_ready, c * KB + (KB + 2))
                    pe.wait_ge(lg_ready, c + 1)
                    for k, (a, b) in enumerate(PRODUCTS):
                        for j in range(KB):
                            last = nc.tensor.matmul(lg_ps[j * DH:(j + 1) * DH, :], gate_w[:, a, j, :], xt[:, u, b, j, :],
                                                    start=(k == 0), stop=(k == len(PRODUCTS) - 1))
                    last.then_inc(lg_made, 1)
                    for m in range(MB):
                        group(c, m, lambda a, j: qk_w[:, a, j, m * P:(m + 1) * P], lambda b, j: xt[:, u, b, j, :])
                    if more:
                        turn(c + 1, 1 - u)
                    for t in range(TT):
                        group(c, MB + t, lambda a, j: xt[:, u, a, j, t * P:(t + 1) * P], lambda b, j: v_w[:, b, j, :])
                    pe.wait_ge(lg_ready, c + 2)
                    pe.wait_ge(lt_summed, c + 1)
                    for t in range(TT):
                        last = nc.tensor.transpose(lt_ps[:, t * P:(t + 1) * P], lg_sb[:, t * P:(t + 1) * P], ident[:, :])
                    last.then_inc(lt_made, 1)
                    for t in range(TT):
                        group(c, MB + TT + t, lambda a, j: xt[:, u, a, j, t * P:(t + 1) * P], lambda b, j: exp_w[:, b, j, :])

                turn(0, 0)
                with pe.Fori(0, PAIRS - 1) as i:
                    chunk(i * 2, 0, True)
                    chunk(i * 2 + 1, 1, True)
                chunk(NCH - 2, 0, True)
                chunk(NCH - 1, 1, False)


def route(nc, g):
    NT = g["NT"]
    logits, gate = g["logits"], g["gate"]
    with ExitStack() as ctx:
        def sb(name, shape, dt):
            return ctx.enter_context(nc.sbuf_tensor(name, shape, dt))

        shape = [P, NT, EXPERTS]
        probs = sb("gate_probs", shape, F32)
        work = sb("work", shape, F32)
        onehot = sb("onehot", shape, F32)
        onehot16 = sb("onehot16", shape, BF16)
        totals = sb("totals", shape, F32)
        places = sb("places", shape, F32)
        ones_row = sb("ones_row", [P, NT], F32)
        prefix = sb("prefix", [P, P], F32)
        prefix16 = sb("prefix16", [P, P], BF16)
        all16 = sb("all16", [P, P], BF16)
        rank = sb("rank", [P, EXPERTS], F32)
        top = sb("top", [P, NT], F32)
        total = sb("total", [P, NT], F32)
        first = sb("first", [P, NT], F32)
        taken = sb("taken", [P, NT], F32)
        here_ps = ctx.enter_context(nc.psum_tensor("here_ps", [P, NT * EXPERTS], F32))
        all_ps = ctx.enter_context(nc.psum_tensor("all_ps", [P, NT * EXPERTS], F32))
        consts_in = ctx.enter_context(nc.semaphore("consts_in"))
        shifted = ctx.enter_context(nc.semaphore("shifted"))
        exp_ready = ctx.enter_context(nc.semaphore("exp_ready"))
        chosen = ctx.enter_context(nc.semaphore("chosen"))
        counted = ctx.enter_context(nc.semaphore("counted"))
        dve_step = ctx.enter_context(nc.semaphore("dve_step"))

        def wide(a):
            return a.unsqueeze(2).to_broadcast(shape)

        with nc.Block() as block:
            @block.sync
            def _(sp):
                sp.dma_start(prefix[:, :], g["prefix_c"]).then_inc(consts_in, 16)
                sp.dma_start(rank[:, :], g["rank_c"]).then_inc(consts_in, 16)
                sp.wait_ge(consts_in, 32)

            @block.scalar
            def _(act):
                act.wait_ge(shifted, 1)
                nc.scalar.activation(probs[:, :, :], work[:, :, :], ACT.Exp).then_inc(exp_ready, 1)

            @block.tensor
            def _(pe):
                pe.wait_ge(chosen, 1)
                rhs = onehot16[:, :, :].rearrange("p t e -> p (t e)")
                nc.tensor.matmul(here_ps[:, :], prefix16[:, :], rhs, start=True, stop=True)
                nc.tensor.matmul(all_ps[:, :], all16[:, :], rhs, start=True, stop=True).then_inc(counted, 1)

            @block.vector
            def _(dve):
                steps = [0]

                def after(ins):
                    steps[0] += 1
                    ins.then_inc(dve_step, 1)
                    dve.wait_ge(dve_step, steps[0])

                V = nc.vector
                V.memset(all16[:, :], 1.0)
                V.memset(ones_row[:, :], 1.0)
                after(V.reduce_max(top[:, :], logits[:, :, :], AX.X))
                V.tensor_tensor(work[:, :, :], logits[:, :, :], wide(top[:, :]), ALU.subtract).then_inc(shifted, 1)
                dve.wait_ge(consts_in, 32)
                V.tensor_copy(prefix16[:, :], prefix[:, :])
                dve.wait_ge(exp_ready, 1)
                V.reduce_sum(total[:, :], probs[:, :, :], AX.X)
                after(V.reduce_max(top[:, :], probs[:, :, :], AX.X))
                after(V.reciprocal(first[:, :], total[:, :]))
                V.tensor_tensor(gate[:, :], top[:, :], first[:, :], ALU.mult)
                after(V.tensor_tensor(onehot[:, :, :], probs[:, :, :], wide(top[:, :]), ALU.is_ge))
                after(V.tensor_tensor(work[:, :, :], onehot[:, :, :], rank[:, :].unsqueeze(1).to_broadcast(shape), ALU.mult))
                after(V.reduce_max(first[:, :], work[:, :, :], AX.X))
                after(V.tensor_tensor(onehot[:, :, :], work[:, :, :], wide(first[:, :]), ALU.is_equal))
                V.tensor_copy(onehot16[:, :, :], onehot[:, :, :]).then_inc(chosen, 1)
                dve.wait_ge(counted, 1)
                after(V.tensor_copy(totals[:, :, :], all_ps[:, :].rearrange("p (t e) -> p t e", e=EXPERTS)))
                for e in range(EXPERTS):
                    last = V.tensor_tensor_scan(places[:, :, e], ones_row[:, :], totals[:, :, e], 0.0, ALU.mult, ALU.add)
                after(last)
                after(V.tensor_tensor(places[:, :, :], places[:, :, :], totals[:, :, :], ALU.subtract))
                after(V.tensor_tensor(places[:, :, :], here_ps[:, :].rearrange("p (t e) -> p t e", e=EXPERTS), places[:, :, :], ALU.add))
                after(V.tensor_scalar(work[:, :, :], places[:, :, :], CAPACITY + 0.5, None, ALU.is_lt))
                after(V.tensor_tensor(work[:, :, :], work[:, :, :], onehot[:, :, :], ALU.mult))
                after(V.reduce_sum(taken[:, :], work[:, :, :], AX.X))
                after(V.tensor_tensor(gate[:, :], gate[:, :], taken[:, :], ALU.mult))


def attend(nc, g):
    QB, CPB, STEPS, UNITS, HQ, DH, SCALE = (g[k] for k in ("QB", "CPB", "STEPS", "UNITS", "HQ", "DH", "SCALE"))
    ident = g["ident"]
    qk_dram, v_dram, a_dram = g["qk_dram"], g["v_dram"], g["a_dram"]
    TT = CH // P
    QT = CH // P
    KROWS = 3 * DH
    XROWS = KROWS + 2
    RP = 8
    GR = HQ * QT * (CPB // 2)
    EXPS = HQ * STEPS
    ON_PE = [4, 7, 10, 13, 15]
    ON_POOL = [s for s in range(STEPS) if s not in ON_PE]
    ADDS = len(ON_POOL) - 1
    INVERT_AT = [15, 20, 22, 29]
    INVERTS = len(INVERT_AT)
    DIVIDE_AT = 8
    READ_SUMS_AT = 7
    READ_DENOMINATORS_AT = 13
    ORDER = ("GGSSVSSGGSSASGSGSCSSGGSSVSGSGSVSGSGSVSSGGSSVGSSVSSGGSASSGVSGSGSVSSGGSVSSVSSGGSS"
             "VSSGGSSVSGSGSAGSSASGGSSVGSSVSSTASSVSSVSS")
    assert [ORDER.count(k) for k in "SGVACT"] == [EXPS, GR, STEPS, len(ON_PE), 1, 1]
    FREE_GR, FREE_PV, FREE_EX = 2 * GR, STEPS, 2

    with ExitStack() as ctx:
        def sb(name, shape, dt):
            return ctx.enter_context(nc.sbuf_tensor(name, shape, dt))

        def pb(name, shape, dt):
            return ctx.enter_context(nc.psum_tensor(name, shape, dt))

        def sem(name):
            return ctx.enter_context(nc.semaphore(name))

        k_max = sb("k_max", [KROWS, HQ, CPB, CH], F16)
        k_exp = sb("k_exp", [XROWS, CPB, HQ, CH], F16)
        q_max = sb("q_max", [KROWS, 2, HQ, CH], F16)
        q_exp = sb("q_exp", [XROWS, 2, HQ, CH], F16)
        v_sb = sb("v_sb", [P, CPB, TT, P], F32)
        probs = sb("probs", [P, RP, HQ, CH], F32)
        acc = sb("acc", [P, 2, HQ, CH], F32)
        ones = sb("ones", [P, DH], F32)
        part = sb("part", [P, 2, GR], F32)
        row_max = sb("row_max", [P, GR // 2], F32)
        max_hi = sb("max_hi", [HQ * QT, 2, P], F16)
        max_lo = sb("max_lo", [HQ * QT, 2, P], F16)
        o_sb = sb("o_sb", [P, 2, CH], F32)
        d_sb = sb("d_sb", [P, 2, CH], F32)
        inv_sb = sb("inv_sb", [P, 2, CH], F32)
        a_sb = sb("a_sb", [P, 2, CH], F32)

        mx = [pb(f"mx{i}", [P, 2 * CH], F32) for i in range(2)]
        ex = [pb(f"ex{i}", [P, CH], F32) for i in range(2)]
        o_ps = pb("o_ps", [P, CH], F32)
        d_ps = pb("d_ps", [P, CH], F32)

        ones_set = sem("ones_set")
        kmax_in = [sem(f"kmax_in{h}") for h in range(HQ)]
        qmax_in = [sem(f"qmax_in{u}") for u in range(2)]
        qexp_in = [sem(f"qexp_in{u}") for u in range(2)]
        kv_in = [sem(f"kv_in{h}") for h in range(2)]
        rows_in = [sem(f"rows_in{u}") for u in range(2)]
        stored = [sem(f"stored{u}") for u in range(2)]
        mx_done = sem("mx_done")
        mx_read = sem("mx_read")
        row_ready = sem("row_ready")
        row_turned = sem("row_turned")
        hi_made = sem("hi_made")
        lo_made = sem("lo_made")
        ex_done = sem("ex_done")
        p_ready = sem("p_ready")
        pv_done = sem("pv_done")
        on_pe = sem("on_pe")
        on_pool = sem("on_pool")
        d_done = sem("d_done")
        o_read = sem("o_read")
        d_read = sem("d_read")
        inverted = sem("inverted")
        divided = sem("divided")

        with nc.Block() as block:
            @block.sync
            def _(sp):
                def halves(dst, src, order, s):
                    for r, half in enumerate(order):
                        sp.dma_start(dst[r * DH:(r + 1) * DH], src[half]).then_inc(s, 16)

                def load_kmax(qb, h):
                    src = qk_dram[qb, 1].rearrange("c l (h d) t -> l h d c t", h=HQ)
                    halves(k_max[:, h, :, :], [src[0, h], src[1, h]], (0, 0, 1), kmax_in[h])

                def load_qmax(qb, c):
                    src = qk_dram[qb, 0, c].rearrange("l (h d) t -> l d h t", h=HQ)
                    halves(q_max[:, c % 2, :, :], [src[0], src[1]], (0, 1, 0), qmax_in[c % 2])

                def load_qexp(qb, c):
                    src = qk_dram[qb, 0, c].rearrange("l (h d) t -> l d h t", h=HQ)
                    halves(q_exp[:, c % 2, :, :], [src[0], src[1]], (0, 1, 0), qexp_in[c % 2])

                def load_kv(qb, half):
                    for c in (2 * half, 2 * half + 1):
                        src = qk_dram[qb, 1, c].rearrange("l (h d) t -> l d h t", h=HQ)
                        halves(k_exp[:, c, :, :], [src[0], src[1]], (0, 0, 1), kv_in[half])
                        sp.dma_start(v_sb[:, c, :, :], v_dram[qb, c]).then_inc(kv_in[half], 16)

                def rows(qb, c):
                    v = qb * CPB + c
                    sp.wait_ge(lo_made, v + 1)
                    for r, src in ((KROWS, max_hi), (KROWS + 1, max_lo)):
                        dst = q_exp[r:r + 1, c % 2, :, :].rearrange("o h (j q) -> o (h j) q", q=P)
                        sp.dma_start(dst, src[:, c % 2, :]).then_inc(rows_in[c % 2], 16)

                def store(v, u):
                    sp.wait_ge(divided, v + 3)
                    sp.dma_start(a_dram[v], a_sb[:, u, :]).then_inc(stored[u], 16)

                def quad(qb, before, more):
                    for c in range(CPB):
                        v = qb * CPB + c
                        sp.wait_ge(o_read, v + 1)
                        load_qexp(qb, c)
                        if c + 1 < CPB or more:
                            sp.wait_ge(mx_read, v * GR + (FREE_GR))
                            if c + 1 < CPB:
                                load_qmax(qb, c + 1)
                            else:
                                load_qmax(qb + 1, 0)
                                for h in range(HQ):
                                    sp.wait_ge(mx_read, v * GR + (FREE_GR + (h + 1) * GR // HQ))
                                    load_kmax(qb + 1, h)
                        if c == 0:
                            sp.wait_ge(pv_done, v * STEPS + (FREE_PV - STEPS // 2))
                            load_kv(qb, 0)
                        rows(qb, c)
                        if c == 0:
                            sp.wait_ge(o_read, v + 2)
                            load_kv(qb, 1)
                        if c >= 2 or before:
                            store(v - 2, c % 2)

                for s in stored:
                    sp.sem_inc(s, 16)
                for h in range(HQ):
                    load_kmax(0, h)
                load_qmax(0, 0)
                quad(0, False, True)
                with sp.Fori(1, QB - 1) as qb:
                    quad(qb, True, True)
                quad(QB - 1, True, False)
                store(UNITS - 2, 0)
                store(UNITS - 1, 1)
                for s in stored:
                    sp.wait_ge(s, 16 * (1 + UNITS // 2))

            @block.vector
            def _(dve):
                dve.sem_inc(mx_read, FREE_GR)
                dve.sem_inc(inverted, 2 * INVERTS)
                nc.vector.memset(ones[:, :], 1.0)
                nc.vector.memset(k_exp[KROWS:XROWS, :, :, :], MSCALE).then_inc(ones_set, 1)

                def invert(v, u, piece):
                    if piece == 0:
                        dve.wait_ge(d_read, v + 2)
                        dve.wait_ge(divided, v + 1)
                    at = slice(piece * CH // INVERTS, (piece + 1) * CH // INVERTS)
                    nc.vector.reciprocal(inv_sb[:, u, at], d_sb[:, u, at]).then_inc(inverted, 1)

                def maxima(v, u, before):
                    for n in range(GR):
                        if n in INVERT_AT and before:
                            invert(v - 2, u, INVERT_AT.index(n))
                        dve.wait_ge(mx_done, v * GR + (n + 1))
                        nc.vector.reduce_max(part[:, u, n:n + 1], mx[(u * (GR + 1) + n) % 2][:, :], AX.X).then_inc(mx_read, 1)
                    dve.wait_ge(mx_read, v * GR + (GR + FREE_GR))
                    nc.vector.tensor_tensor(row_max[:, :], part[:, u, 0:GR:2], part[:, u, 1:GR:2], ALU.max).then_inc(row_ready, 1)
                    turned = mx[(u * (GR + 1) + GR) % 2][0:HQ * QT, 0:P]
                    dve.wait_ge(row_turned, v + 1)
                    nc.vector.tensor_scalar(max_hi[:, u, :], turned, -1.0 / MSCALE, None, ALU.mult).then_inc(hi_made, 1)
                    dve.wait_ge(hi_made, v + 1)
                    nc.vector.scalar_tensor_tensor(out=max_lo[:, u, :], in0=turned, scalar=-1.0 / MSCALE, in1=max_hi[:, u, :],
                                                   op0=ALU.mult, op1=ALU.subtract).then_inc(lo_made, 1)

                maxima(0, 0, False)
                maxima(1, 1, False)
                with dve.Fori(1, UNITS // 2) as i:
                    maxima(i * 2, 0, True)
                    maxima(i * 2 + 1, 1, True)
                for piece in range(INVERTS):
                    invert(UNITS - 2, 0, piece)
                for piece in range(INVERTS):
                    invert(UNITS - 1, 1, piece)

            @block.gpsimd
            def _(pool):
                pool.sem_inc(on_pool, ADDS)
                pool.sem_inc(divided, 2)

                def divide(v, v2, u):
                    pool.wait_ge(o_read, v + 3)
                    pool.wait_ge(inverted, v * INVERTS + 3 * INVERTS)
                    pool.wait_ge(stored[u], v2 * 16 + 16)
                    nc.gpsimd.tensor_tensor(a_sb[:, u, :], o_sb[:, u, :], inv_sb[:, u, :], ALU.mult).then_inc(divided, 1)

                def unit(v, v2, u, before):
                    pool.wait_ge(d_done, v + 1)
                    for n, s in enumerate(ON_POOL[1:]):
                        pool.wait_ge(p_ready, v * EXPS + (FREE_EX + HQ * (s + 1)))
                        a = probs[:, ON_POOL[0] + u * STEPS % RP, :, :] if n == 0 else acc[:, u, :, :]
                        if n:
                            pool.wait_ge(on_pool, v * ADDS + (ADDS + n))
                        nc.gpsimd.tensor_tensor(acc[:, u, :, :], a, probs[:, (u * STEPS + s) % RP, :, :], ALU.add).then_inc(on_pool, 1)
                        if n == DIVIDE_AT and before:
                            divide(v - 1, v2 - (1 - u), 1 - u)

                unit(0, 0, 0, False)
                unit(1, 0, 1, True)
                with pool.Fori(1, UNITS // 2) as i:
                    unit(i * 2, i, 0, True)
                    unit(i * 2 + 1, i, 1, True)
                divide(UNITS - 1, UNITS // 2 - 1, 1)

            @block.scalar
            def _(act):
                act.sem_inc(p_ready, FREE_EX)
                act.sem_inc(o_read, 2)
                act.sem_inc(d_read, 1)

                def read_o(v, u):
                    act.wait_ge(pv_done, v * STEPS + (FREE_PV + STEPS))
                    act.wait_ge(divided, v + 1)
                    nc.scalar.activation(o_sb[:, u, :], o_ps[:, :], ACT.Copy).then_inc(o_read, 1)

                def read_d(v, u):
                    act.wait_ge(d_done, v + 3)
                    act.wait_ge(inverted, v * INVERTS + INVERTS)
                    nc.scalar.activation(d_sb[:, u, :], d_ps[:, :], ACT.Copy).then_inc(d_read, 1)

                def unit(v, u, before):
                    for s in range(STEPS):
                        for h in range(HQ):
                            n = HQ * s + h
                            if n == READ_SUMS_AT and before:
                                read_o(v - 1, 1 - u)
                            if n == READ_DENOMINATORS_AT and before:
                                read_d(v - 1, 1 - u)
                            act.wait_ge(ex_done, v * EXPS + (n + 1))
                            if h == 0:
                                old = s - RP
                                act.wait_ge(pv_done, v * STEPS + (FREE_PV + old + 1))
                                back, at = (1, old + STEPS) if old < 0 else (0, old)
                                if at in ON_PE:
                                    act.wait_ge(on_pe, v * len(ON_PE) + (len(ON_PE) * (1 - back) + ON_PE.index(at) + 1))
                                else:
                                    act.wait_ge(on_pool, v * ADDS + (ADDS * (1 - back) + max(ON_POOL.index(at), 1)))
                            nc.scalar.activation(probs[:, (u * STEPS + s) % RP, h, :], ex[n % 2][:, :], ACT.Exp, scale=SCALE).then_inc(p_ready, 1)

                unit(0, 0, False)
                unit(1, 1, True)
                with act.Fori(1, UNITS // 2) as i:
                    unit(i * 2, 0, True)
                    unit(i * 2 + 1, 1, True)
                read_o(UNITS - 1, 1)
                read_d(UNITS - 1, 1)

            @block.tensor
            def _(pe):
                pe.sem_inc(pv_done, FREE_PV)
                pe.sem_inc(on_pe, len(ON_PE))
                pe.sem_inc(d_done, 2)
                pe.wait_ge(ones_set, 1)

                def max_group(v, v2, v4, u, n, first):
                    h, j, half = n // (2 * QT), n // 2 % QT, n % 2
                    if n == 0:
                        pe.wait_ge(qmax_in[u], (v2 + 1) * (3 * 16))
                    if n % (2 * QT) == 0:
                        pe.wait_ge(kmax_in[h], (v4 + 1) * (3 * 16))
                    if n != 1:
                        pe.wait_ge(mx_read, v * GR + (FREE_GR + n - 1 if n else FREE_GR))
                    elif not first:
                        pe.wait_ge(lo_made, v)
                    bank = mx[(u * (GR + 1) + n) % 2]
                    for k in range(2):
                        last = nc.tensor.matmul(bank[:, k * CH:(k + 1) * CH], q_max[:, u, h, j * P:(j + 1) * P], k_max[:, h, 2 * half + k, :],
                                                start=True, stop=True)
                    last.then_inc(mx_done, 1)

                def turn_rows(v, u):
                    pe.wait_ge(row_ready, v + 1)
                    bank = mx[(u * (GR + 1) + GR) % 2]
                    nc.tensor.transpose(bank[0:HQ * QT, 0:P], row_max[:, :], ident[:, :]).then_inc(row_turned, 1)

                def scores(v, u, s, h):
                    n = HQ * s + h
                    pe.wait_ge(p_ready, v * EXPS + (n + 1))
                    nc.tensor.matmul(ex[n % 2][:, :], k_exp[:, s // TT, h, s % TT * P:(s % TT + 1) * P], q_exp[:, u, h, :],
                                     start=True, stop=True).then_inc(ex_done, 1)

                def sums(v, u, s):
                    pe.wait_ge(p_ready, v * EXPS + (FREE_EX + HQ * (s + 1)))
                    if s == 0:
                        pe.wait_ge(o_read, v + 2)
                    for h in range(HQ):
                        last = nc.tensor.matmul(o_ps[h * DH:(h + 1) * DH, :], v_sb[:, s // TT, s % TT, h * DH:(h + 1) * DH],
                                                probs[:, (u * STEPS + s) % RP, h, :], start=(s == 0), stop=(s == STEPS - 1))
                    last.then_inc(pv_done, 1)

                def add_up(v, u, s):
                    if s == ON_PE[0]:
                        pe.wait_ge(d_read, v + 1)
                    for h in range(HQ):
                        last = nc.tensor.matmul(d_ps[h * DH:(h + 1) * DH, :], ones[:, :], probs[:, (u * STEPS + s) % RP, h, :],
                                                start=(s == ON_PE[0]), stop=False)
                    last.then_inc(on_pe, 1)

                def close(v, u):
                    pe.wait_ge(on_pool, v * ADDS + 2 * ADDS)
                    for h in range(HQ):
                        last = nc.tensor.matmul(d_ps[h * DH:(h + 1) * DH, :], ones[:, :], acc[:, u, h, :], start=False, stop=True)
                    last.then_inc(d_done, 1)

                def unit(v, v2, v4, w2, w4, u, before, after):
                    n_scores = n_groups = n_sums = n_adds = 0
                    for work in ORDER:
                        if work == "S":
                            s, h = divmod(n_scores, HQ)
                            if n_scores == 0:
                                pe.wait_ge(qexp_in[u], (v2 + 1) * (3 * 16))
                                pe.wait_ge(rows_in[u], (v2 + 1) * (2 * 16))
                            if n_scores % (EXPS // 2) == 0:
                                pe.wait_ge(kv_in[s // (STEPS // 2)], (v4 + 1) * (8 * 16))
                            scores(v, u, s, h)
                            n_scores += 1
                        elif work == "G":
                            if after:
                                max_group(v + 1, w2, w4, 1 - u, n_groups, False)
                            n_groups += 1
                        elif work == "V":
                            if n_sums:
                                sums(v, u, n_sums - 1)
                            elif before:
                                sums(v - 1, 1 - u, STEPS - 1)
                            n_sums += 1
                        elif work == "A":
                            if n_adds:
                                add_up(v, u, ON_PE[n_adds - 1])
                            elif before:
                                add_up(v - 1, 1 - u, ON_PE[-1])
                            n_adds += 1
                        elif work == "C" and before:
                            close(v - 1, 1 - u)
                        elif work == "T" and after:
                            turn_rows(v + 1, 1 - u)

                def pair(i, before=True, after=True):
                    v = i * 2
                    unit(v, i, v // CPB, i, (v + 1) // CPB, 0, before, True)
                    unit(v + 1, i, (v + 1) // CPB, i + 1, (v + 2) // CPB, 1, True, after)

                for n in range(GR):
                    max_group(0, 0, 0, 0, n, True)
                turn_rows(0, 0)
                pair(0, before=False)
                with pe.Fori(1, UNITS // 2 - 1) as i:
                    pair(i)
                pair(UNITS // 2 - 1, after=False)
                sums(UNITS - 1, 1, STEPS - 1)
                add_up(UNITS - 1, 1, STEPS - 1)
                close(UNITS - 1, 1)


def finish_rows(nc, g):
    B, CPB, QUADS, D, NCH = (g[k] for k in ("B", "CPB", "QUADS", "D", "NCH"))
    TT = CH // P
    RING = 4
    w_out_sb, b_out_sb, gate = g["w_out_sb"], g["b_out_sb"], g["gate"]
    with ExitStack() as ctx:
        def sb(name, shape, dt):
            return ctx.enter_context(nc.sbuf_tensor(name, shape, dt))

        def sem(name):
            return ctx.enter_context(nc.semaphore(name))

        a_in = sb("a_in", [P, 2, QUADS, CH], F32)
        x_in = sb("x_in", [P, 2, TT, D], F32)
        y_in = sb("y_in", [P, 2, TT, D], F32)
        g_now = sb("g_now", [P, 2, TT], F32)
        o_out = sb("o_out", [P, 2, TT, D], F32)
        prod = [ctx.enter_context(nc.psum_tensor(f"prod{i}", [P, D], F32)) for i in range(RING)]
        loaded = [sem(f"loaded{u}") for u in range(2)]
        out_stored = [sem(f"out_stored{u}") for u in range(2)]
        gates = sem("gates")
        biased = sem("biased")
        multiplied = sem("multiplied")
        gated = sem("gated")
        summed = sem("summed")

        with nc.Block() as block:
            @block.sync
            def _(sp):
                for s in out_stored:
                    sp.sem_inc(s, 16)
                a_view = g["a_dram"].rearrange("(b q c) p t -> b c p q t", b=B, q=QUADS)
                rows = [t.rearrange("(b c t p) d -> b c p t d", b=B, c=CPB, t=TT) for t in (g["x_rows"], g["y_dram"], g["out_rows"])]
                with sp.Fori(0, B) as b:
                    with sp.Fori(0, CPB // 2) as ci:
                        for u in range(2):
                            c = b * CPB + ci * 2 + u
                            sp.wait_ge(summed, c + 1)
                            ch = ci * 2 + u
                            sp.dma_start(a_in[:, u, :, :], a_view[b, ch]).then_inc(loaded[u], 16)
                            sp.dma_start(y_in[:, u, :, :], rows[1][b, ch]).then_inc(loaded[u], 16)
                            sp.dma_start(x_in[:, u, :, :], rows[0][b, ch]).then_inc(loaded[u], 16)

            @block.scalar
            def _(act):
                view = g["out_rows"].rearrange("(i u t p) d -> i u p t d", u=2, t=TT, p=P)
                with act.Fori(0, NCH // 2) as i:
                    for u in range(2):
                        act.wait_ge(summed, i * 2 + (u + 3))
                        act.dma_start(view[i, u], o_out[:, u, :, :]).then_inc(out_stored[u], 16)
                for s in out_stored:
                    act.wait_ge(s, 16 * (1 + NCH // 2))

            @block.gpsimd
            def _(pool):
                with pool.Fori(0, NCH // 2) as i:
                    for u in range(2):
                        pool.wait_ge(loaded[u], i * 48 + 48)
                        nc.gpsimd.tensor_tensor(x_in[:, u, :, :], x_in[:, u, :, :],
                                                b_out_sb[:, :].unsqueeze(1).to_broadcast([P, TT, D]), ALU.add).then_inc(biased, 1)

            @block.tensor
            def _(pe):
                with pe.Fori(0, NCH // 2) as i:
                    for u in range(2):
                        pe.wait_ge(loaded[u], i * 48 + 48)
                        for t in range(TT):
                            pe.wait_ge(gated, (i * 2 + u) * TT + (t + 1))
                            for q in range(QUADS):
                                last = nc.tensor.matmul(prod[t][:, :], a_in[:, u, q, t * P:(t + 1) * P], w_out_sb[:, q, :],
                                                        start=(q == 0), stop=(q == QUADS - 1))
                            last.then_inc(multiplied, 1)

            @block.vector
            def _(dve):
                dve.sem_inc(gated, RING)
                dve.sem_inc(summed, 2)
                with dve.Fori(0, NCH // 2) as i:
                    for u in range(2):
                        c = i * 2 + u
                        nc.vector.tensor_copy(g_now[:, u, :], gate[:, bass.ds(c * TT, TT)]).then_inc(gates, 1)
                        dve.wait_ge(loaded[u], i * 48 + 48)
                        dve.wait_ge(gates, c + 1)
                        dve.wait_ge(out_stored[u], i * 16 + 16)
                        for t in range(TT):
                            dve.wait_ge(multiplied, c * TT + (t + 1))
                            nc.vector.scalar_tensor_tensor(out=o_out[:, u, t, :], in0=y_in[:, u, t, :], scalar=g_now[:, u, t:t + 1],
                                                           in1=prod[t][:, :], op0=ALU.mult, op1=ALU.add).then_inc(gated, 1)
                        dve.wait_ge(biased, c + 1)
                        dve.wait_ge(gated, c * TT + (TT + RING))
                        nc.vector.tensor_tensor(o_out[:, u, :, :], o_out[:, u, :, :], x_in[:, u, :, :], ALU.add).then_inc(summed, 1)


_INS = ["L0_attn_x", "L0_attn_w_qkv", "L0_attn_w_out", "L0_attn_b_out", "L0_attn_mask_logits",
        "L0_ffn_w_gate", "L0_ffn_w_expert", "L0_ffn_b_expert"]


def _constants():
    import numpy as np
    dh, heads = 32, 4
    n = np.arange(dh)
    rows = [np.sqrt((1.0 if f in (0, dh // 2) else 2.0) / dh) * np.cos(2 * np.pi * f * n / dh) for f in range(dh // 2 + 1)]
    rows += [np.sqrt(2.0 / dh) * np.sin(2 * np.pi * f * n / dh) for f in range(1, dh // 2)]
    basis = np.kron(np.eye(heads), np.stack(rows)).astype(np.float32)
    prefix = np.triu(np.ones((P, P))).astype(np.float32)
    rank = np.tile(np.arange(EXPERTS, 0, -1), (P, 1)).astype(np.float32)
    return {"ident": np.eye(P, dtype=np.float32), "basis": basis, "prefix": prefix, "rank": rank}


def kernel(**inputs):
    import numpy as np
    import concourse.bacc as bacc
    from concourse.bass_utils import run_bass_kernel_spmd

    nc = bacc.Bacc("TRN2", target_bir_lowering=False, num_devices=1)
    arrays, args = {}, []
    for name, a in [(n, inputs[n]) for n in _INS] + list(_constants().items()):
        a = np.ascontiguousarray(a)
        arrays[f"in_{name}"] = a
        args.append(nc.dram_tensor(f"in_{name}", a.shape, mybir.dt.from_np(a.dtype), kind="ExternalInput").ap())
    out = nc.dram_tensor("out_0", inputs["L0_attn_x"].shape, F32, kind="ExternalOutput").ap()
    attention_and_experts_kernel(nc, *args, out)
    r = run_bass_kernel_spmd(nc, [arrays], core_ids=[0])
    return r.results[0]["out_0"]
```

```python
from contextlib import ExitStack

import concourse.bass as bass
from concourse import mybir

F32 = mybir.dt.float32
F16 = mybir.dt.float16
BF16 = mybir.dt.bfloat16
ALU = mybir.AluOpType
ACT = mybir.ActivationFunctionType
AX = mybir.AxisListType

P = 128
CH = 512
EXPERTS = 8
CAPACITY = 100
EPS = 1e-5
XSCALE = 2.0 ** 10
WTOP = 2.0 ** 14
VSCALE = 2.0 ** 5
MSCALE = 256.0


def attention_and_experts_kernel(nc, x, w_qkv, w_out, b_out, mask_logits, w_gate, w_expert, b_expert,
                                 ident_c, basis_c, prefix_c, rank_c, token_c, place_c, out):
    B, S, D = x.shape
    DH = 32
    NF = mask_logits.shape[0]
    HQ = P // DH
    QUADS = D // P
    KB = D // P
    TT = CH // P
    CPB = S // CH
    NCH = B * CPB
    QB = B * QUADS
    NT = B * S // P
    STEPS = S // P
    UNITS = QB * CPB
    SCALE = float(DH) ** -0.5
    assert D == CH and DH == 32 and NF == DH // 2 + 1

    x_rows = x.rearrange("b s d -> (b s) d")
    out_rows = out.rearrange("b s d -> (b s) d")
    qk_dram = nc.dram_tensor("qk_scratch", (QB, 2, CPB, 2, P, CH), F16).ap()
    v_dram = nc.dram_tensor("v_scratch", (QB, CPB, P, TT, P), F32).ap()
    base_dram = nc.dram_tensor("base_scratch", (B * S, D), F32).ap()
    inv_dram = nc.dram_tensor("inverse_scratch", (UNITS, HQ, CH), F32).ap()
    a_dram = nc.dram_tensor("attn_scratch", (UNITS, P, CH), F32).ap()

    with ExitStack() as whole:
        def keep(name, shape, dt):
            return whole.enter_context(nc.sbuf_tensor(name, shape, dt))

        ident = keep("ident", [P, P], F32)
        out_w = keep("out_w", [P, 2, QUADS, D], F16)
        v_power = keep("v_power", [P, 1], F32)
        out_scale = keep("out_scale", [P, 1], F32)
        b_out_sb = keep("b_out_sb", [P, D], F32)
        logits = keep("logits", [P, NT, EXPERTS], F32)
        prefix = keep("prefix", [P, P], F32)
        rank = keep("rank", [P, EXPERTS], F32)
        token_part = keep("token_part", [P, 2, NT], F32)
        place = keep("place", [P, CAPACITY], F32)

        project(nc, locals())
        with ExitStack() as attention:
            k_max = attention.enter_context(nc.sbuf_tensor("k_max", [3 * DH, HQ, CPB, CH], F16))
            q_max = attention.enter_context(nc.sbuf_tensor("q_max", [3 * DH, 2, HQ, CH], F16))
            part = attention.enter_context(nc.sbuf_tensor("part", [P, 2, HQ * TT * CPB // 2], F32))
            mx = [attention.enter_context(nc.psum_tensor(f"mx{i}", [P, 2 * CH], F32)) for i in range(2)]
            route(nc, locals())
            attend(nc, locals())
        finish_rows(nc, locals())


def project(nc, g):
    D, DH, NF, HQ, QUADS, KB, TT, CPB, NCH = (g[k] for k in ("D", "DH", "NF", "HQ", "QUADS", "KB", "TT", "CPB", "NCH"))
    B = g["B"]
    ident, logits = g["ident"], g["logits"]
    MB = 2 * D // P
    QK_RING, V_RING, MM_RING = 4, 2, 4
    PRODUCTS = [(0, 0), (0, 1), (1, 0)]
    GROUPS = MB + TT

    with ExitStack() as ctx:
        def sb(name, shape, dt):
            return ctx.enter_context(nc.sbuf_tensor(name, shape, dt))

        def pb(name, shape, dt):
            return ctx.enter_context(nc.psum_tensor(name, shape, dt))

        def sem(name):
            return ctx.enter_context(nc.semaphore(name))

        w_qkv_sb = sb("w_qkv_sb", [P, KB, 3 * D], F32)
        w_filt = sb("w_filt", [P, KB, 2 * D], F32)
        qk_w = sb("qk_w", [P, 2, KB, 2 * D], F16)
        v_w = sb("v_w", [P, 2, KB, D], F16)
        gate_w = sb("gate_w", [P, 2, KB, DH], F16)
        w_max = sb("w_max", [P, 4], F32)
        w_top = sb("w_top", [P, 4], F32)
        power = sb("power", [P, 4], F32)
        w_scale = sb("w_scale", [P, 4], F32)
        w_inv = sb("w_inv", [P, 4], F32)
        balance = sb("balance", [P, 4], F32)
        w_gate_sb = sb("w_gate_sb", [P, KB, DH], F32)
        basis = sb("basis", [P, P], F32)
        basis_m = sb("basis_m", [P, P], F32)
        filt = sb("filt", [P, P], F32)
        mask = sb("mask", [P, 3], F32)
        eps = sb("eps", [P, 1], F32)
        wt = sb("wt", [P, 2, D], F32)
        xs = sb("xs", [P, 2, TT, D], F32)
        xt = sb("xt", [P, 2, 2, KB, CH], F16)
        stats = sb("stats", [P, TT, 6], F32)
        mean_var = sb("mean_var", [P, TT, 2], F32)
        std = sb("std", [P, TT], F32)
        rstd = sb("rstd", [P, TT], F32)
        qk_out = sb("qk_out", [P, QK_RING, 2, CH], F16)
        v_out = sb("v_out", [P, V_RING, D], F32)
        lg_sb = sb("lg_sb", [P, CH], F32)

        mm = [pb(f"mm{i}", [P, CH], F32) for i in range(MM_RING)]
        xt_ps = [pb(f"xt_ps{i}", [P, CH], F32) for i in range(2)]
        lg_ps = pb("lg_ps", [P, CH], F32)
        lt_ps = pb("lt_ps", [P, CH], F32)

        weights_in = sem("weights_in")
        zeroed = sem("zeroed")
        ident_in = sem("ident_in")
        mask_in = sem("mask_in")
        consts_in = sem("consts_in")
        mask_exp = sem("mask_exp")
        mask_step = sem("mask_step")
        basis_ready = sem("basis_ready")
        filt_made = sem("filt_made")
        filt_ready = sem("filt_ready")
        wt_made = sem("wt_made")
        wt_ready = sem("wt_ready")
        wf_made = sem("wf_made")
        wf_ready = sem("wf_ready")
        w_maxed = sem("w_maxed")
        w_topped = sem("w_topped")
        ratio_ready = sem("ratio_ready")
        root_ready = sem("root_ready")
        dve_step = sem("dve_step")

        x_in = [sem(f"x_in{u}") for u in range(2)]
        x_turned = sem("x_turned")
        varied = sem("varied")
        stats_seen = sem("stats_seen")
        aggregated = sem("aggregated")
        std_ready = sem("std_ready")
        rstd_ready = sem("rstd_ready")
        xn_ready = sem("xn_ready")
        xt_made = sem("xt_made")
        xt_high = sem("xt_high")
        xt_ready = sem("xt_ready")
        lg_made = sem("lg_made")
        lg_ready = sem("lg_ready")
        lt_made = sem("lt_made")
        lt_summed = sem("lt_summed")
        mm_done = sem("mm_done")
        hi_ready = sem("hi_ready")
        lo_ready = sem("lo_ready")
        v_ready = sem("v_ready")
        copied = sem("copied")
        qk_stored = [sem(f"qk_stored{i}") for i in range(QK_RING)]
        v_stored = [sem(f"v_stored{i}") for i in range(V_RING)]
        PAIRS = NCH // 2

        scaled = sem("scaled")
        eps_set = sem("eps_set")
        w_halved = sem("w_halved")
        w_balanced = sem("w_balanced")
        w_split = sem("w_split")
        WEIGHT_LOADS = 3

        with nc.Block() as block:
            @block.gpsimd
            def _(pool):
                x_view = g["x_rows"].rearrange("(i u t p) d -> i u p t d", u=2, t=TT, p=P)
                nc.gpsimd.dma_start(xs[:, 0, :, :], x_view[0, 0]).then_inc(x_in[0], 16)
                for n, (a, b) in enumerate(((0, 2), (2, 4))):
                    pool.wait_ge(w_maxed, n + 1)
                    nc.gpsimd.partition_all_reduce(w_top[:, a:b], w_max[:, a:b], P, bass.bass_isa.ReduceOp.max).then_inc(w_topped, 1)
                    if n == 0:
                        nc.gpsimd.dma_start(xs[:, 1, :, :], x_view[0, 1]).then_inc(x_in[1], 16)
                with pool.Fori(1, PAIRS) as i:
                    for u in range(2):
                        pool.wait_ge(x_turned, i * 2 + (u + 1))
                        nc.gpsimd.dma_start(xs[:, u, :, :], x_view[i, u]).then_inc(x_in[u], 16)

            @block.sync
            def _(sp):
                sp.dma_start(ident[:, :], g["ident_c"]).then_inc(ident_in, 16)
                sp.dma_start(w_qkv_sb[:, :, :], g["w_qkv"].rearrange("(j p) n -> p j n", p=P)).then_inc(weights_in, 16)
                sp.dma_start(basis[:, :], g["basis_c"]).then_inc(weights_in, 16)
                sp.wait_ge(zeroed, 1)
                sp.dma_start(w_gate_sb[:, :, 0:EXPERTS], g["w_gate"].rearrange("(j p) n -> p j n", p=P)).then_inc(weights_in, 16)
                for dst, src in ((g["b_out_sb"][:, :], g["b_out"].partition_broadcast(P)), (g["prefix"][:, :], g["prefix_c"]),
                                 (g["rank"][:, :], g["rank_c"]), (g["token_part"][:, :, :], g["token_c"]), (g["place"][:, :], g["place_c"])):
                    sp.dma_start(dst, src).then_inc(consts_in, 16)
                sp.wait_ge(consts_in, 5 * 16)
                for s in (*qk_stored, *v_stored):
                    sp.sem_inc(s, 16)
                x_view, base_view = (t.rearrange("(b c r) d -> b c r d", b=B, c=CPB) for t in (g["x_rows"], g["base_dram"]))
                with sp.Fori(0, B) as b:
                    with sp.Fori(0, CPB // 2) as ci:
                        for u in range(2):
                            c = b * CPB + ci * 2 + u
                            ch = ci * 2 + u
                            for m in range(MB):
                                sp.wait_ge(lo_ready, c * MB + (m + 1))
                                dst = g["qk_dram"].rearrange("(b q) k c l p t -> b q k c p l t", b=B)[b, m % QUADS, m // QUADS, ch]
                                sp.dma_start(dst, qk_out[:, m % QK_RING, :, :]).then_inc(qk_stored[m % QK_RING], 16)
                            sp.dma_start(base_view[b, ch], x_view[b, ch]).then_inc(copied, 16)
                            for t in range(TT):
                                sp.wait_ge(v_ready, c * TT + (t + 1 + TT))
                                dst = g["v_dram"].rearrange("(b q) c p t n -> b c t p q n", b=B)[b, ch, t]
                                sp.dma_start(dst, v_out[:, t % V_RING, :].rearrange("p (q n) -> p q n", q=QUADS)).then_inc(v_stored[t % V_RING], 16)
                for s in qk_stored:
                    sp.wait_ge(s, 16 * (1 + NCH * MB // QK_RING))
                for s in v_stored:
                    sp.wait_ge(s, 16 * (1 + NCH * TT // V_RING))
                sp.wait_ge(copied, 16 * NCH)

            @block.scalar
            def _(act):
                act.sem_inc(lg_ready, 1)
                ml = g["mask_logits"].rearrange("(f o) -> f o", o=1)
                for h in range(HQ):
                    act.dma_start(mask[h * DH:h * DH + NF, 0:1], ml).then_inc(mask_in, 16)
                    act.dma_start(mask[h * DH + NF:(h + 1) * DH, 0:1], ml[1:NF - 1, :]).then_inc(mask_in, 16)
                act.wait_ge(eps_set, 1)
                act.sem_inc(v_ready, TT)

                def high_half(halves, w, n):
                    nc.scalar.activation(halves[:, 0], w, ACT.Copy, scale=w_scale[:, n:n + 1]).then_inc(w_split, 1)

                def deviation(c):
                    act.wait_ge(aggregated, c + 1)
                    nc.scalar.activation(std[:, :], mean_var[:, :, 1], ACT.Sqrt, bias=eps[:, 0:1], scale=XSCALE ** -2).then_inc(std_ready, 1)

                def turned(c, u):
                    for j in range(KB):
                        act.wait_ge(xt_made, c * KB + (j + 1))
                        nc.scalar.activation(xt[:, u, 0, j, :], xt_ps[j % 2][:, :], ACT.Copy).then_inc(xt_high, 1)

                def chunk(c, u, more):
                    act.wait_ge(lg_made, c + 1)
                    act.wait_ge(lt_made, c + 1)
                    nc.scalar.activation(lg_sb[:, :], lg_ps[:, :], ACT.Copy, scale=w_inv[:, 1:2]).then_inc(lg_ready, 1)
                    for m in range(MB):
                        act.wait_ge(mm_done, c * GROUPS + (m + 1))
                        act.wait_ge(qk_stored[m % QK_RING], (c * (MB // QK_RING) + (m // QK_RING + 1)) * 16)
                        nc.scalar.activation(qk_out[:, m % QK_RING, 0, :], mm[m % MM_RING][:, :], ACT.Copy,
                                             scale=w_inv[:, 2 + m // QUADS:3 + m // QUADS]).then_inc(hi_ready, 1)
                        if m == 5 and more:
                            deviation(c + 1)
                    if more:
                        turned(c + 1, 1 - u)
                    for t in range(TT):
                        act.wait_ge(mm_done, c * GROUPS + (MB + t + 1))
                        act.wait_ge(v_stored[t % V_RING], (c * (TT // V_RING) + (t // V_RING + 1)) * 16)
                        nc.scalar.activation(v_out[:, t % V_RING, :], mm[(MB + t) % MM_RING][:, :], ACT.Copy, scale=VSCALE / (WTOP * XSCALE)).then_inc(v_ready, 1)

                deviation(0)
                turned(0, 0)
                act.wait_ge(mask_in, 2 * HQ * 16)
                nc.scalar.activation(mask[:, 1:2], mask[:, 0:1], ACT.Exp, scale=-1.0).then_inc(mask_exp, 1)
                for m in range(MB):
                    act.wait_ge(wf_made, m + 1)
                    nc.scalar.activation(w_filt[:, :, m * P:(m + 1) * P],
                                         mm[m % 2][:, :].rearrange("p (j n) -> p j n", j=KB), ACT.Copy).then_inc(wf_ready, 1)
                    if m == 2:
                        act.wait_ge(scaled, 1)
                        high_half(v_w, w_qkv_sb[:, :, 2 * D:3 * D], 0)
                        high_half(gate_w, w_gate_sb[:, :, :], 1)
                act.wait_ge(scaled, 2)
                for n in range(2):
                    high_half(qk_w[:, :, :, n * D:(n + 1) * D], w_filt[:, :, n * D:(n + 1) * D], 2 + n)
                act.wait_ge(ratio_ready, 1)
                nc.scalar.activation(balance[:, 1:2], balance[:, 0:1], ACT.Sqrt).then_inc(root_ready, 1)
                act.wait_ge(w_balanced, 1)
                with act.Fori(0, PAIRS - 1) as i:
                    chunk(i * 2, 0, True)
                    chunk(i * 2 + 1, 1, True)
                chunk(NCH - 2, 0, True)
                chunk(NCH - 1, 1, False)

            @block.vector
            def _(dve):
                nc.vector.memset(w_gate_sb[:, :, :], 0.0).then_inc(zeroed, 1)
                nc.vector.memset(eps[:, :], EPS / XSCALE ** 2).then_inc(eps_set, 1)
                dve.sem_inc(lt_summed, 1)
                dve.sem_inc(xt_ready, 2)

                def low_halves(c, u):
                    for j in range(KB):
                        dve.wait_ge(xt_high, c * KB + (j + 1))
                        nc.vector.tensor_tensor(xt[:, u, 1, j, :], xt_ps[j % 2][:, :], xt[:, u, 0, j, :], ALU.subtract).then_inc(xt_ready, 1)

                def moments(c, c2, u):
                    dve.wait_ge(x_in[u], (c2 + 1) * 16)
                    for t in range(TT):
                        last = nc.vector.bn_stats(stats[:, t, :], xs[:, u, t, :])
                    last.then_inc(varied, 1)
                    dve.wait_ge(varied, c + 1)
                    dve.sem_inc(stats_seen, 1)
                    for t in range(TT):
                        last = nc.vector.bn_aggr(mean_var[:, t, :], stats[:, t, :])
                    last.then_inc(aggregated, 1)

                def normalise(c, u):
                    dve.wait_ge(std_ready, c + 1)
                    nc.vector.reciprocal(rstd[:, :], std[:, :]).then_inc(rstd_ready, 1)
                    dve.wait_ge(rstd_ready, c + 1)
                    for t in range(TT):
                        last = nc.vector.tensor_scalar(xs[:, u, t, :], xs[:, u, t, :], mean_var[:, t, 0:1], rstd[:, t:t + 1],
                                                       ALU.subtract, ALU.mult)
                    last.then_inc(xn_ready, 1)

                def chunk(c, c2, u, more):
                    for m in range(MB):
                        dve.wait_ge(hi_ready, c * MB + (m + 1))
                        nc.vector.scalar_tensor_tensor(out=qk_out[:, m % QK_RING, 1, :], in0=mm[m % MM_RING][:, :],
                                                       scalar=w_inv[:, 2 + m // QUADS:3 + m // QUADS], in1=qk_out[:, m % QK_RING, 0, :],
                                                       op0=ALU.mult, op1=ALU.subtract).then_inc(lo_ready, 1)
                        if m == 3 and more:
                            moments(c + 1, c2 + u, 1 - u)
                        if m == 5 and more:
                            normalise(c + 1, 1 - u)
                    if more:
                        low_halves(c + 1, 1 - u)
                    dve.wait_ge(lt_made, c + 2)
                    nc.vector.tensor_reduce(out=logits[:, bass.ds(c * TT, TT), :],
                                            in_=lt_ps[:, :].rearrange("p (t j e) -> p t e j", t=TT, j=KB)[:, :, 0:EXPERTS, :],
                                            op=ALU.add, axis=AX.X).then_inc(lt_summed, 1)

                steps = [0]

                def after(ins):
                    steps[0] += 1
                    ins.then_inc(dve_step, 1)
                    dve.wait_ge(dve_step, steps[0])

                def largest(n, w):
                    return nc.vector.tensor_reduce(out=w_max[:, n:n + 1], in_=w, op=ALU.max, axis=AX.XY, apply_absolute_value=True)

                def scales(a, b):
                    after(nc.vector.tensor_scalar_max(power[:, a:b], w_top[:, a:b], 2.0 ** -100))
                    bits = power[:, a:b].bitcast(mybir.dt.int32)
                    after(nc.vector.tensor_scalar(bits, bits, 0x7F800000, None, ALU.bitwise_and))
                    after(nc.vector.reciprocal(w_scale[:, a:b], power[:, a:b]))
                    nc.vector.tensor_scalar(w_inv[:, a:b], power[:, a:b], 1.0 / (WTOP * XSCALE), None, ALU.mult)
                    nc.vector.tensor_scalar(w_scale[:, a:b], w_scale[:, a:b], WTOP, None, ALU.mult).then_inc(scaled, 1)
                    dve.wait_ge(scaled, 1 + a // 2)

                def low_half(halves, w, n):
                    dve.wait_ge(w_split, n + 1)
                    return nc.vector.scalar_tensor_tensor(out=halves[:, 1], in0=w, scalar=w_scale[:, n:n + 1], in1=halves[:, 0],
                                                          op0=ALU.mult, op1=ALU.subtract)

                moments(0, 0, 0)
                normalise(0, 0)
                low_halves(0, 0)
                dve.wait_ge(weights_in, 16 * WEIGHT_LOADS)
                dve.wait_ge(mask_exp, 1)
                nc.vector.tensor_scalar_add(mask[:, 2:3], mask[:, 1:2], 1.0).then_inc(mask_step, 1)
                dve.wait_ge(mask_step, 1)
                nc.vector.reciprocal(mask[:, 1:2], mask[:, 2:3]).then_inc(mask_step, 1)
                dve.wait_ge(mask_step, 2)
                nc.vector.tensor_scalar(basis_m[:, :], basis[:, :], mask[:, 1:2], None, ALU.mult).then_inc(basis_ready, 1)
                largest(0, w_qkv_sb[:, :, 2 * D:3 * D])
                largest(1, w_gate_sb[:, :, :]).then_inc(w_maxed, 1)
                dve.wait_ge(filt_made, 1)
                nc.vector.tensor_copy(filt[:, :], lg_ps[:, 0:P]).then_inc(filt_ready, 1)
                for m in range(MB):
                    dve.wait_ge(wt_made, m + 1)
                    if m >= 2:
                        dve.wait_ge(wf_made, m - 1)
                    nc.vector.tensor_copy(wt[:, m % 2, :], xt_ps[m % 2][:, :]).then_inc(wt_ready, 1)
                    if m == 1:
                        dve.wait_ge(w_topped, 1)
                        scales(0, 2)
                        nc.vector.tensor_copy(g["v_power"][:, :], power[:, 0:1])
                    if m == 5:
                        low_half(v_w, w_qkv_sb[:, :, 2 * D:3 * D], 0)
                        low_half(gate_w, w_gate_sb[:, :, :], 1).then_inc(w_halved, 1)
                    if m == MB - 2:
                        dve.wait_ge(wf_ready, QUADS)
                        largest(2, w_filt[:, :, 0:D])
                dve.wait_ge(wf_ready, MB)
                largest(3, w_filt[:, :, D:2 * D]).then_inc(w_maxed, 1)
                dve.wait_ge(w_topped, 2)
                scales(2, 4)
                for n in range(2):
                    last = low_half(qk_w[:, :, :, n * D:(n + 1) * D], w_filt[:, :, n * D:(n + 1) * D], 2 + n)
                last.then_inc(w_halved, 1)
                after(nc.vector.reciprocal(balance[:, 2:3], power[:, 2:3]))
                after(nc.vector.tensor_tensor(balance[:, 3:4], power[:, 3:4], balance[:, 2:3], ALU.mult))
                nc.vector.tensor_scalar(balance[:, 0:1], balance[:, 3:4], 2.0 ** -100, 2.0 ** 100, ALU.max, ALU.min).then_inc(ratio_ready, 1)
                dve.wait_ge(root_ready, 1)
                bits = balance[:, 1:2].bitcast(mybir.dt.int32)
                after(nc.vector.tensor_scalar(bits, bits, 0x7F800000, None, ALU.bitwise_and))
                after(nc.vector.reciprocal(balance[:, 2:3], balance[:, 1:2]))
                nc.vector.tensor_tensor(w_inv[:, 2:4], w_inv[:, 2:4], balance[:, 1:3], ALU.mult).then_inc(w_balanced, 1)
                dve.wait_ge(w_balanced, 1)

                with dve.Fori(0, PAIRS - 1) as i:
                    chunk(i * 2, i, 0, True)
                    chunk(i * 2 + 1, i, 1, True)
                chunk(NCH - 2, PAIRS - 1, 0, True)
                chunk(NCH - 1, PAIRS - 1, 1, False)

            @block.tensor
            def _(pe):
                pe.sem_inc(x_turned, 2)
                pe.sem_inc(lt_made, 1)

                def turn(c, u):
                    pe.wait_ge(xn_ready, c + 1)
                    for j in range(KB):
                        pe.wait_ge(xt_ready, c * KB + (j + 1))
                        for t in range(TT):
                            last = nc.tensor.transpose(xt_ps[j % 2][:, t * P:(t + 1) * P], xs[:, u, t, j * P:(j + 1) * P], ident[:, :])
                        last.then_inc(xt_made, 1)
                    pe.wait_ge(xt_ready, c * KB + (KB + 2))
                    pe.sem_inc(x_turned, 1)

                def group(c, n, lhs, rhs):
                    if n < MM_RING:
                        pe.wait_ge(v_ready, c * TT + (n + 1))
                    else:
                        pe.wait_ge(lo_ready, c * MB + (n - MM_RING + 1))
                    for j in range(KB):
                        for k, (a, b) in enumerate(PRODUCTS):
                            last = nc.tensor.matmul(mm[n % MM_RING][:, :], lhs(a, j), rhs(b, j), start=(j == k == 0),
                                                    stop=(j == KB - 1 and k == len(PRODUCTS) - 1))
                    last.then_inc(mm_done, 1)

                def chunk(c, u, more):
                    pe.wait_ge(xt_ready, c * KB + (KB + 2))
                    pe.wait_ge(lg_ready, c + 1)
                    for k, (a, b) in enumerate(PRODUCTS):
                        for j in range(KB):
                            last = nc.tensor.matmul(lg_ps[j * DH:(j + 1) * DH, :], gate_w[:, a, j, :], xt[:, u, b, j, :],
                                                    start=(k == 0), stop=(k == len(PRODUCTS) - 1))
                    last.then_inc(lg_made, 1)
                    for m in range(MB):
                        group(c, m, lambda a, j: qk_w[:, a, j, m * P:(m + 1) * P], lambda b, j: xt[:, u, b, j, :])
                    if more:
                        turn(c + 1, 1 - u)
                    for t in range(TT):
                        group(c, MB + t, lambda a, j: xt[:, u, a, j, t * P:(t + 1) * P], lambda b, j: v_w[:, b, j, :])
                    pe.wait_ge(lg_ready, c + 2)
                    pe.wait_ge(lt_summed, c + 1)
                    for t in range(TT):
                        last = nc.tensor.transpose(lt_ps[:, t * P:(t + 1) * P], lg_sb[:, t * P:(t + 1) * P], ident[:, :])
                    last.then_inc(lt_made, 1)

                pe.wait_ge(ident_in, 16)
                turn(0, 0)
                pe.wait_ge(weights_in, 16 * WEIGHT_LOADS)
                pe.wait_ge(basis_ready, 1)
                nc.tensor.matmul(lg_ps[:, 0:P], basis_m[:, :], basis[:, :], start=True, stop=True).then_inc(filt_made, 1)

                def turn_weights(m):
                    if m >= 2:
                        pe.wait_ge(wt_ready, m - 1)
                    for j in range(KB):
                        last = nc.tensor.transpose(xt_ps[m % 2][:, j * P:(j + 1) * P], w_qkv_sb[:, j, m * P:(m + 1) * P], ident[:, :])
                    last.then_inc(wt_made, 1)

                turn_weights(0)
                pe.wait_ge(filt_ready, 1)
                for m in range(MB):
                    if m + 1 < MB:
                        turn_weights(m + 1)
                    pe.wait_ge(wt_ready, m + 1)
                    if m >= 2:
                        pe.wait_ge(wf_ready, m - 1)
                    for j in range(KB):
                        last = nc.tensor.matmul(mm[m % 2][:, j * P:(j + 1) * P], wt[:, m % 2, j * P:(j + 1) * P], filt[:, :],
                                                start=True, stop=True, skip_group_check=True)
                    last.then_inc(wf_made, 1)

                pe.wait_ge(w_split, 4)
                pe.wait_ge(w_halved, 2)
                with pe.Fori(0, PAIRS - 1) as i:
                    chunk(i * 2, 0, True)
                    chunk(i * 2 + 1, 1, True)
                chunk(NCH - 2, 0, True)
                chunk(NCH - 1, 1, False)


def route(nc, g):
    NT, KB, D = g["NT"], g["KB"], g["D"]
    N_TOKENS = NT * P
    logits, ident, prefix, rank, token_part, place = (g[k] for k in ("logits", "ident", "prefix", "rank", "token_part", "place"))
    GATE_PARTS = 3
    GROUPS = g["HQ"] * g["TT"] * g["CPB"] // 2
    PER_EXPERT = GROUPS // EXPERTS
    FIELDS = 2 + GATE_PARTS
    with ExitStack() as ctx:
        def sb(name, shape, dt):
            return ctx.enter_context(nc.sbuf_tensor(name, shape, dt))

        def pb(name, shape, dt):
            return ctx.enter_context(nc.psum_tensor(name, shape, dt))

        def sem(name):
            return ctx.enter_context(nc.semaphore(name))

        shape = [P, NT, EXPERTS]
        probs = sb("gate_probs", shape, F32)
        work = sb("work", shape, F32)
        onehot = sb("onehot", shape, F32)
        onehot16 = sb("onehot16", shape, BF16)
        totals = sb("totals", shape, F32)
        places = sb("places", shape, F32)
        ones_row = sb("ones_row", [P, NT], F32)
        prefix16 = sb("prefix16", [P, P], BF16)
        all16 = sb("all16", [P, P], BF16)
        top = sb("top", [P, NT], F32)
        total = sb("total", [P, NT], F32)
        first = sb("first", [P, NT], F32)
        gate = sb("gate", [P, NT], F32)
        in_queue = sb("in_queue", [P, NT], F32)
        rest = sb("rest", [P, GATE_PARTS - 1, NT], F32)
        gate_part = sb("gate_part", [P, GATE_PARTS, NT], BF16)
        at_place = sb("at_place", [P, NT, CAPACITY], BF16)
        to_slot = sb("to_slot", [P, NT, FIELDS, EXPERTS], BF16)
        fields = sb("fields", [CAPACITY, FIELDS, EXPERTS], F32)
        number = sb("number", [CAPACITY, EXPERTS], F32)
        empty = sb("empty", [CAPACITY, EXPERTS], F32)
        index = sb("index", [CAPACITY, EXPERTS], mybir.dt.uint32)
        slot_gate = sb("slot_gate", [CAPACITY, EXPERTS], F32)
        x_slot = sb("x_slot", [CAPACITY, EXPERTS, D], F32)
        xn_slot = sb("xn_slot", [CAPACITY, EXPERTS, D], F32)
        xt_slot = sb("xt_slot", [P, 2, KB, CAPACITY], F32)
        o_slot = sb("o_slot", [CAPACITY, 2, D], F32)
        stats = sb("slot_stats", [CAPACITY, EXPERTS, 6], F32)
        mean_var = sb("slot_mean_var", [CAPACITY, EXPERTS, 2], F32)
        std = sb("slot_std", [CAPACITY, EXPERTS], F32)
        rstd = sb("slot_rstd", [CAPACITY, EXPERTS], F32)
        eps = sb("slot_eps", [P, 1], F32)
        w_exp_sb = sb("w_exp_sb", [P, KB, D], F32)
        b_exp_sb = sb("b_exp_sb", [P, D], F32)
        w_out_sb = sb("w_out_sb", [P, KB, D], F32)
        w_max = sb("w_out_max", [P, 1], F32)
        w_top = sb("w_out_top", [P, 1], F32)
        w_power = sb("w_out_power", [P, 1], F32)
        w_scale = sb("w_out_scale", [P, 1], F32)
        turn_ps = [pb(f"turn_ps{i}", [P, CH], F32) for i in range(2)]
        prod_ps = [pb(f"prod_ps{i}", [P, D], F32) for i in range(2)]
        here_ps, all_ps, slot_ps = turn_ps[0], turn_ps[1], prod_ps[0]
        assert NT * EXPERTS <= CH

        w_out_in = sem("w_out_in")
        w_exp_in = sem("w_exp_in")
        queries_in = sem("queries_in")
        keys_in = sem("keys_in")
        first_max_done = sem("first_max_done")
        first_max_read = sem("first_max_read")
        shifted = sem("shifted")
        exp_ready = sem("exp_ready")
        chosen = sem("chosen")
        counted = sem("counted")
        dve_step = sem("dve_step")
        listed = sem("listed")
        queued = sem("queued")
        cleared = sem("cleared")
        indexed = sem("indexed")
        gathered = [sem(f"gathered{e}") for e in range(EXPERTS)]
        aggregated = sem("slot_aggregated")
        std_ready = sem("slot_std_ready")
        normalised = sem("normalised")
        turned = sem("turned")
        turned_sb = sem("turned_sb")
        product = sem("product")
        weighed = sem("weighed")
        w_maxed = sem("w_out_maxed")
        w_topped = sem("w_out_topped")
        scattered = [sem(f"scattered{i}") for i in range(2)]

        def wide(a):
            return a.unsqueeze(2).to_broadcast(shape)

        with nc.Block() as block:
            @block.sync
            def _(sp):
                sp.dma_start(w_out_sb[:, :, :], g["w_out"].rearrange("(j p) n -> p j n", p=P)).then_inc(w_out_in, 16)
                sp.dma_start(w_exp_sb[:, :, :], g["w_expert"].rearrange("(j p) n -> p j n", p=P)).then_inc(w_exp_in, 16)
                sp.dma_start(b_exp_sb[:, :], g["b_expert"].partition_broadcast(P)).then_inc(w_exp_in, 16)
                load_queries(sp, g, g["q_max"][:, 0, :, :], 0, 0, queries_in)
                for h in range(g["HQ"]):
                    load_head_for_maxima(sp, g, 0, h, keys_in)
                sp.wait_ge(w_out_in, 16)
                sp.wait_ge(w_exp_in, 32)

            @block.gpsimd
            def _(pool):
                nc.gpsimd.memset(x_slot[:, :, :], 0.0).then_inc(cleared, 1)
                pool.wait_ge(cleared, 1)
                pool.wait_ge(w_maxed, 1)
                nc.gpsimd.partition_all_reduce(w_top[:, :], w_max[:, :], P, bass.bass_isa.ReduceOp.max).then_inc(w_topped, 1)
                pool.wait_ge(indexed, 1)
                for e in range(EXPERTS):
                    pool.indirect_dma_start(x_slot[:, e, :], None, g["x_rows"], bass.IndirectOffsetOnAxis(index[:, e:e + 1], 0),
                                            bounds_check=N_TOKENS - 1, oob_is_err=False).then_inc(gathered[e], 16)
                for e in range(EXPERTS):
                    pool.wait_ge(weighed, e + 1)
                    pool.indirect_dma_start(g["base_dram"], bass.IndirectOffsetOnAxis(index[:, e:e + 1], 0), o_slot[:, e % 2, :], None,
                                            bounds_check=N_TOKENS - 1, oob_is_err=False).then_inc(scattered[e % 2], 16)
                for s in scattered:
                    pool.wait_ge(s, 16 * EXPERTS // 2)

            @block.scalar
            def _(act):
                act.wait_ge(shifted, 1)
                nc.scalar.activation(probs[:, :, :], work[:, :, :], ACT.Exp).then_inc(exp_ready, 1)
                act.wait_ge(aggregated, 1)
                nc.scalar.activation(std[:, :], mean_var[:, :, 1], ACT.Sqrt, bias=eps[0:CAPACITY, 0:1]).then_inc(std_ready, 1)
                for e in range(EXPERTS):
                    act.wait_ge(turned, e + 1)
                    if e >= 2:
                        act.wait_ge(product, e - 1)
                    nc.scalar.activation(xt_slot[:, e % 2, :, :],
                                         turn_ps[e % 2][:, 0:KB * CAPACITY].rearrange("p (j n) -> p j n", j=KB), ACT.Copy).then_inc(turned_sb, 1)

            @block.tensor
            def _(pe):
                pe.wait_ge(chosen, 1)
                rhs = onehot16[:, :, :].rearrange("p t e -> p (t e)")
                nc.tensor.matmul(here_ps[:, :], prefix16[:, :], rhs, start=True, stop=True)
                nc.tensor.matmul(all_ps[:, :], all16[:, :], rhs, start=True, stop=True).then_inc(counted, 1)
                pe.wait_ge(listed, 1)
                for t in range(NT):
                    last = nc.tensor.matmul(slot_ps[0:CAPACITY, 0:FIELDS * EXPERTS], at_place[:, t, :],
                                            to_slot[:, t, :, :].rearrange("p k e -> p (k e)"), start=(t == 0), stop=(t == NT - 1))
                last.then_inc(queued, 1)

                def turn(e):
                    pe.wait_ge(normalised, e + 1)
                    if e >= 2:
                        pe.wait_ge(turned_sb, e - 1)
                    for j in range(KB):
                        last = nc.tensor.transpose(turn_ps[e % 2][:, j * CAPACITY:(j + 1) * CAPACITY], xn_slot[:, e, j * P:(j + 1) * P],
                                                   ident[0:CAPACITY, 0:CAPACITY])
                    last.then_inc(turned, 1)

                pe.wait_ge(w_exp_in, 32)
                pe.wait_ge(queries_in, 3 * 16)
                pe.wait_ge(keys_in, g["HQ"] * 3 * 16)
                turn(0)
                for e in range(EXPERTS):
                    if e + 1 < EXPERTS:
                        turn(e + 1)
                    pe.wait_ge(turned_sb, e + 1)
                    if e >= 2:
                        pe.wait_ge(weighed, e - 1)
                    for j in range(KB):
                        last = nc.tensor.matmul(prod_ps[e % 2][0:CAPACITY, :], xt_slot[:, e % 2, j, :], w_exp_sb[:, j, :],
                                                start=(j == 0), stop=(j == KB - 1))
                        if j == KB - 1:
                            last.then_inc(product, 1)
                        for n in range(e * PER_EXPERT + j * PER_EXPERT // KB, e * PER_EXPERT + (j + 1) * PER_EXPERT // KB):
                            if n >= 2:
                                pe.wait_ge(first_max_read, n - 1)
                            scores_for_maxima(nc, g, g["mx"][n % 2], 0, n).then_inc(first_max_done, 1)

            @block.vector
            def _(dve):
                steps = [0]

                def after(ins):
                    steps[0] += 1
                    ins.then_inc(dve_step, 1)
                    dve.wait_ge(dve_step, steps[0])

                V = nc.vector
                V.memset(all16[:, :], 1.0)
                V.memset(ones_row[:, :], 1.0)
                V.memset(eps[:, :], EPS)
                after(V.reduce_max(top[:, :], logits[:, :, :], AX.X))
                V.tensor_tensor(work[:, :, :], logits[:, :, :], wide(top[:, :]), ALU.subtract).then_inc(shifted, 1)
                V.tensor_copy(prefix16[:, :], prefix[:, :])
                dve.wait_ge(exp_ready, 1)
                V.reduce_sum(total[:, :], probs[:, :, :], AX.X)
                after(V.reduce_max(top[:, :], probs[:, :, :], AX.X))
                after(V.reciprocal(first[:, :], total[:, :]))
                V.tensor_tensor(gate[:, :], top[:, :], first[:, :], ALU.mult)
                after(V.tensor_tensor(onehot[:, :, :], probs[:, :, :], wide(top[:, :]), ALU.is_ge))
                after(V.tensor_tensor(work[:, :, :], onehot[:, :, :], rank[:, :].unsqueeze(1).to_broadcast(shape), ALU.mult))
                after(V.reduce_max(first[:, :], work[:, :, :], AX.X))
                after(V.tensor_tensor(onehot[:, :, :], work[:, :, :], wide(first[:, :]), ALU.is_equal))
                V.tensor_copy(onehot16[:, :, :], onehot[:, :, :]).then_inc(chosen, 1)
                dve.wait_ge(counted, 1)
                after(V.tensor_copy(totals[:, :, :], all_ps[:, :].rearrange("p (t e) -> p t e", e=EXPERTS)))
                for e in range(EXPERTS):
                    last = V.tensor_tensor_scan(places[:, :, e], ones_row[:, :], totals[:, :, e], 0.0, ALU.mult, ALU.add)
                after(last)
                after(V.tensor_tensor(places[:, :, :], places[:, :, :], totals[:, :, :], ALU.subtract))
                after(V.tensor_tensor(places[:, :, :], here_ps[:, :].rearrange("p (t e) -> p t e", e=EXPERTS), places[:, :, :], ALU.add))
                after(V.tensor_tensor(places[:, :, :], places[:, :, :], onehot[:, :, :], ALU.mult))
                after(V.reduce_sum(in_queue[:, :], places[:, :, :], AX.X))
                wide_place = [P, NT, CAPACITY]
                V.tensor_tensor(at_place[:, :, :], place[:, :].unsqueeze(1).to_broadcast(wide_place),
                                in_queue[:, :].unsqueeze(2).to_broadcast(wide_place), ALU.is_equal)
                for k in range(2):
                    V.tensor_tensor(to_slot[:, :, k, :], onehot[:, :, :], wide(token_part[:, k, :]), ALU.mult)
                left = gate[:, :]
                for k in range(GATE_PARTS):
                    after(V.tensor_copy(gate_part[:, k, :], left))
                    if k + 1 < GATE_PARTS:
                        after(V.tensor_tensor(rest[:, k, :], left, gate_part[:, k, :], ALU.subtract))
                        left = rest[:, k, :]
                for k in range(GATE_PARTS):
                    last = V.tensor_tensor(to_slot[:, :, 2 + k, :], onehot[:, :, :], wide(gate_part[:, k, :]), ALU.mult)
                last.then_inc(listed, 1)
                dve.wait_ge(w_out_in, 16)
                V.tensor_reduce(out=w_max[:, :], in_=w_out_sb[:, :, :], op=ALU.max, axis=AX.XY, apply_absolute_value=True).then_inc(w_maxed, 1)
                dve.wait_ge(queued, 1)
                after(V.tensor_copy(fields[:, :, :], slot_ps[0:CAPACITY, 0:FIELDS * EXPERTS].rearrange("p (k e) -> p k e", e=EXPERTS)))
                V.tensor_tensor(slot_gate[:, :], fields[:, 3, :], fields[:, 4, :], ALU.add)
                after(V.tensor_tensor(number[:, :], fields[:, 0, :], fields[:, 1, :], ALU.add))
                V.tensor_tensor(slot_gate[:, :], fields[:, 2, :], slot_gate[:, :], ALU.add)
                after(V.tensor_scalar(empty[:, :], number[:, :], 0.0, 4.0 * N_TOKENS, ALU.is_equal, ALU.mult))
                after(V.tensor_tensor(number[:, :], number[:, :], empty[:, :], ALU.add))
                V.tensor_scalar(index[:, :], number[:, :], -1.0, None, ALU.add).then_inc(indexed, 1)

                def finish(e):
                    dve.wait_ge(product, e + 1)
                    if e >= 2:
                        dve.wait_ge(scattered[e % 2], 16 * (e // 2))
                    rows = o_slot[:, e % 2, :]
                    after(V.tensor_tensor(rows, prod_ps[e % 2][0:CAPACITY, :], b_exp_sb[0:CAPACITY, :], ALU.add))
                    V.scalar_tensor_tensor(out=rows, in0=rows, scalar=slot_gate[:, e:e + 1], in1=x_slot[:, e, :],
                                           op0=ALU.mult, op1=ALU.add).then_inc(weighed, 1)

                dve.wait_ge(w_topped, 1)
                after(V.tensor_scalar_max(w_power[:, :], w_top[:, :], 2.0 ** -100))
                bits = w_power[:, :].bitcast(mybir.dt.int32)
                after(V.tensor_scalar(bits, bits, 0x7F800000, None, ALU.bitwise_and))
                after(V.reciprocal(w_scale[:, :], w_power[:, :]))
                V.scalar_tensor_tensor(out=g["out_scale"][:, :], in0=w_power[:, :], scalar=1.0 / (WTOP * VSCALE), in1=g["v_power"][:, :],
                                       op0=ALU.mult, op1=ALU.mult)
                after(V.tensor_scalar(w_scale[:, :], w_scale[:, :], WTOP, None, ALU.mult))
                after(V.tensor_scalar(g["out_w"][:, 0], w_out_sb[:, :, :], w_scale[:, 0:1], None, ALU.mult))
                V.scalar_tensor_tensor(out=g["out_w"][:, 1], in0=w_out_sb[:, :, :], scalar=w_scale[:, 0:1], in1=g["out_w"][:, 0],
                                       op0=ALU.mult, op1=ALU.subtract)

                for e in range(EXPERTS):
                    dve.wait_ge(gathered[e], 16)
                    last = V.bn_stats(stats[:, e, :], x_slot[:, e, :])
                after(last)
                for e in range(EXPERTS):
                    last = V.bn_aggr(mean_var[:, e, :], stats[:, e, :])
                last.then_inc(aggregated, 1)
                dve.wait_ge(std_ready, 1)
                after(V.reciprocal(rstd[:, :], std[:, :]))
                for e in range(EXPERTS):
                    V.tensor_scalar(xn_slot[:, e, :], x_slot[:, e, :], mean_var[:, e, 0:1], rstd[:, e:e + 1],
                                    ALU.subtract, ALU.mult).then_inc(normalised, 1)
                for e in range(EXPERTS):
                    for n in range(e * PER_EXPERT, (e + 1) * PER_EXPERT):
                        dve.wait_ge(first_max_done, n + 1)
                        V.reduce_max(g["part"][:, 0, n:n + 1], g["mx"][n % 2][:, :], AX.X).then_inc(first_max_read, 1)
                        if n == e * PER_EXPERT and e:
                            finish(e - 1)
                finish(EXPERTS - 1)


def load_halves(sp, dst, src, order, loaded):
    rows = dst.shape[0] // len(order)
    for r, half in enumerate(order):
        sp.dma_start(dst[r * rows:(r + 1) * rows], src[half]).then_inc(loaded, 16)


def load_head_for_maxima(sp, g, qb, h, loaded):
    src = g["qk_dram"][qb, 1].rearrange("c l (h d) t -> l h d c t", h=g["HQ"])
    load_halves(sp, g["k_max"][:, h, :, :], [src[0, h], src[1, h]], (0, 0, 1), loaded)


def load_queries(sp, g, dst, qb, c, loaded):
    src = g["qk_dram"][qb, 0, c].rearrange("l (h d) t -> l d h t", h=g["HQ"])
    load_halves(sp, dst, [src[0], src[1]], (0, 1, 0), loaded)


def scores_for_maxima(nc, g, bank, u, n):
    h, j, half = n // (2 * g["TT"]), n // 2 % g["TT"], n % 2
    for k in range(2):
        last = nc.tensor.matmul(bank[:, k * CH:(k + 1) * CH], g["q_max"][:, u, h, j * P:(j + 1) * P], g["k_max"][:, h, 2 * half + k, :],
                                start=True, stop=True)
    return last


def attend(nc, g):
    QB, CPB, STEPS, UNITS, HQ, DH, SCALE = (g[k] for k in ("QB", "CPB", "STEPS", "UNITS", "HQ", "DH", "SCALE"))
    ident = g["ident"]
    qk_dram, v_dram, a_dram, inv_dram = g["qk_dram"], g["v_dram"], g["a_dram"], g["inv_dram"]
    k_max, q_max, part, mx = g["k_max"], g["q_max"], g["part"], g["mx"]
    TT = CH // P
    QT = CH // P
    KROWS = 3 * DH
    XROWS = KROWS + 2
    RP = 8
    GR = HQ * QT * (CPB // 2)
    EXPS = HQ * STEPS
    ON_DVE = [5, 8, 11]
    ON_PE = ["sum", 14, 15]
    ON_POOL = [s for s in range(STEPS) if s not in ON_DVE + ON_PE]
    ADDS = len(ON_POOL) - 1
    DVE_ADDS_AT = [24, 26, 28, 30]
    INVERT_AT = 15
    DIVIDE_AT = 6
    READ_SUMS_AT = 10
    READ_DENOMINATORS_AT = 11
    ORDER = ("GGVSSGSSGSGSASSGGSSCSGSGSVSSGGSSVSSGGSSVSGSGSVSGSGSVSGSGSVSSGGSSVSSGGSSVGSSVSSG"
             "GSSVSSGGSSVSSVSSGGSSVSSGGSSVSSASSTASVS")
    assert [ORDER.count(k) for k in "SGVACT"] == [EXPS, GR, STEPS, len(ON_PE), 1, 1]
    FREE_GR, FREE_PV, FREE_EX = 2 * GR, STEPS, 2

    with ExitStack() as ctx:
        def sb(name, shape, dt):
            return ctx.enter_context(nc.sbuf_tensor(name, shape, dt))

        def pb(name, shape, dt):
            return ctx.enter_context(nc.psum_tensor(name, shape, dt))

        def sem(name):
            return ctx.enter_context(nc.semaphore(name))

        k_exp = sb("k_exp", [XROWS, CPB, HQ, CH], F16)
        q_exp = sb("q_exp", [XROWS, 2, HQ, CH], F16)
        v_sb = sb("v_sb", [P, CPB, TT, P], F32)
        probs = sb("probs", [P, RP, HQ, CH], F32)
        acc = sb("acc", [P, 2, HQ, CH], F32)
        dve_acc = sb("dve_acc", [P, HQ, CH], F32)
        ones = sb("ones", [P, DH], F32)
        row_max = sb("row_max", [P, GR // 2], F32)
        max_hi = sb("max_hi", [HQ * QT, 2, P], F16)
        max_lo = sb("max_lo", [HQ * QT, 2, P], F16)
        o_sb = sb("o_sb", [P, 2, CH], F32)
        d_sb = sb("d_sb", [P, 2, CH], F32)
        d_dense = sb("d_dense", [P, HQ * CH // P], F32)
        inv_dense = sb("inv_dense", [P, HQ * CH // P], F32)
        inv_sb = sb("inv_sb", [P, 2, CH], F32)
        a_sb = sb("a_sb", [P, 2, CH], F32)

        ex = [pb(f"ex{i}", [P, CH], F32) for i in range(2)]
        o_ps = pb("o_ps", [P, CH], F32)
        d_ps = pb("d_ps", [P, CH], F32)

        ones_set = sem("ones_set")
        kmax_in = [sem(f"kmax_in{h}") for h in range(HQ)]
        qmax_in = [sem(f"qmax_in{u}") for u in range(2)]
        qexp_in = [sem(f"qexp_in{u}") for u in range(2)]
        kv_in = [sem(f"kv_in{h}") for h in range(2)]
        rows_in = [sem(f"rows_in{u}") for u in range(2)]
        stored = [sem(f"stored{u}") for u in range(2)]
        mx_done = sem("mx_done")
        mx_read = sem("mx_read")
        row_ready = sem("row_ready")
        row_turned = sem("row_turned")
        hi_made = sem("hi_made")
        lo_made = sem("lo_made")
        ex_done = sem("ex_done")
        p_ready = sem("p_ready")
        pv_done = sem("pv_done")
        on_pe = sem("on_pe")
        on_dve = sem("on_dve")
        dense_in = sem("dense_in")
        inv_stored = sem("inv_stored")
        inv_in = sem("inv_in")
        on_pool = sem("on_pool")
        d_done = sem("d_done")
        o_read = sem("o_read")
        d_read = sem("d_read")
        inverted = sem("inverted")
        divided = sem("divided")

        with nc.Block() as block:
            @block.sync
            def _(sp):
                def load_kmax(qb, h):
                    load_head_for_maxima(sp, g, qb, h, kmax_in[h])

                def load_qmax(qb, c):
                    load_queries(sp, g, q_max[:, c % 2, :, :], qb, c, qmax_in[c % 2])

                def load_qexp(qb, c):
                    load_queries(sp, g, q_exp[0:KROWS, c % 2, :, :], qb, c, qexp_in[c % 2])

                def load_kv(qb, half):
                    for c in (2 * half, 2 * half + 1):
                        src = qk_dram[qb, 1, c].rearrange("l (h d) t -> l d h t", h=HQ)
                        load_halves(sp, k_exp[0:KROWS, c, :, :], [src[0], src[1]], (0, 0, 1), kv_in[half])
                        sp.dma_start(v_sb[:, c, :, :], v_dram[qb, c]).then_inc(kv_in[half], 16)

                def rows(qb, c):
                    v = qb * CPB + c
                    sp.wait_ge(lo_made, v + 1)
                    for r, src in ((KROWS, max_hi), (KROWS + 1, max_lo)):
                        dst = q_exp[r:r + 1, c % 2, :, :].rearrange("o h (j q) -> o (h j) q", q=P)
                        sp.dma_start(dst, src[:, c % 2, :]).then_inc(rows_in[c % 2], 16)

                def store(v, u):
                    sp.wait_ge(divided, v + 3)
                    sp.dma_start(a_dram[v], a_sb[:, u, :]).then_inc(stored[u], 16)

                def denominators(v, u):
                    sp.wait_ge(d_read, v + 2)
                    for h in range(HQ):
                        sp.dma_start(d_dense[h * DH:(h + 1) * DH, :], d_sb[h * DH:h * DH + 1, u, :].rearrange("o (r n) -> o r n", r=DH)).then_inc(dense_in, 16)
                    sp.wait_ge(inverted, v + 3)
                    sp.dma_start(inv_dram[v].rearrange("h (r n) -> (h r) n", r=DH), inv_dense[:, :]).then_inc(inv_stored, 16)
                    sp.wait_ge(inv_stored, v * 16 + 16)
                    for h in range(HQ):
                        sp.dma_start(inv_sb[h * DH:(h + 1) * DH, u, :], inv_dram[v, h].partition_broadcast(DH)).then_inc(inv_in, 16)

                def quad(qb, before, more):
                    for c in range(CPB):
                        v = qb * CPB + c
                        sp.wait_ge(o_read, v + 1)
                        load_qexp(qb, c)
                        if c >= 2 or before:
                            denominators(v - 2, c % 2)
                        if c + 1 < CPB or more:
                            sp.wait_ge(mx_read, v * GR + (FREE_GR))
                            if c + 1 < CPB:
                                load_qmax(qb, c + 1)
                            else:
                                load_qmax(qb + 1, 0)
                                for h in range(HQ):
                                    sp.wait_ge(mx_read, v * GR + (FREE_GR + (h + 1) * GR // HQ))
                                    load_kmax(qb + 1, h)
                        if c == 0:
                            sp.wait_ge(pv_done, v * STEPS + (FREE_PV - STEPS // 2))
                            load_kv(qb, 0)
                        rows(qb, c)
                        if c == 0:
                            sp.wait_ge(o_read, v + 2)
                            load_kv(qb, 1)
                        if c >= 2 or before:
                            store(v - 2, c % 2)

                for s in stored:
                    sp.sem_inc(s, 16)
                for s in (*kmax_in, qmax_in[0]):
                    sp.sem_inc(s, 3 * 16)
                quad(0, False, True)
                with sp.Fori(1, QB - 1) as qb:
                    quad(qb, True, True)
                quad(QB - 1, True, False)
                denominators(UNITS - 2, 0)
                denominators(UNITS - 1, 1)
                store(UNITS - 2, 0)
                store(UNITS - 1, 1)
                for s in stored:
                    sp.wait_ge(s, 16 * (1 + UNITS // 2))

            @block.vector
            def _(dve):
                dve.sem_inc(mx_read, FREE_GR + GR)
                dve.sem_inc(inverted, 2)
                dve.sem_inc(on_dve, len(DVE_ADDS_AT))

                def invert(v):
                    dve.wait_ge(dense_in, v * (HQ * 16) + HQ * 16)
                    nc.vector.reciprocal(inv_dense[:, :], d_dense[:, :]).then_inc(inverted, 1)

                def add(v, u, piece):
                    k, heads = piece // 2 + 1, slice(piece % 2 * 2, piece % 2 * 2 + 2)
                    s = ON_DVE[k]
                    dve.wait_ge(p_ready, v * EXPS + (FREE_EX + HQ * s + heads.stop))
                    if piece == 0:
                        dve.wait_ge(on_pe, v * len(ON_PE) + 1)
                    if k > 1:
                        dve.wait_ge(on_dve, v * len(DVE_ADDS_AT) + (len(DVE_ADDS_AT) + piece - 1))
                    a = dve_acc[:, heads, :] if k > 1 else probs[:, (u * STEPS + ON_DVE[0]) % RP, heads, :]
                    nc.vector.tensor_tensor(dve_acc[:, heads, :], a, probs[:, (u * STEPS + s) % RP, heads, :], ALU.add).then_inc(on_dve, 1)

                def maxima(v, u, before, grouped=True):
                    for n in range(GR if grouped else 0):
                        if n == INVERT_AT and before:
                            invert(v - 2)
                        if n in DVE_ADDS_AT:
                            add(v - 1, 1 - u, DVE_ADDS_AT.index(n))
                        dve.wait_ge(mx_done, v * GR + (n + 1))
                        nc.vector.reduce_max(part[:, u, n:n + 1], mx[(u * (GR + 1) + n) % 2][:, :], AX.X).then_inc(mx_read, 1)
                    dve.wait_ge(mx_read, v * GR + (GR + FREE_GR))
                    nc.vector.tensor_tensor(row_max[:, :], part[:, u, 0:GR:2], part[:, u, 1:GR:2], ALU.max).then_inc(row_ready, 1)
                    turned = mx[(u * (GR + 1) + GR) % 2][0:HQ * QT, 0:P]
                    dve.wait_ge(row_turned, v + 1)
                    nc.vector.tensor_scalar(max_hi[:, u, :], turned, -1.0 / MSCALE, None, ALU.mult).then_inc(hi_made, 1)
                    dve.wait_ge(hi_made, v + 1)
                    nc.vector.scalar_tensor_tensor(out=max_lo[:, u, :], in0=turned, scalar=-1.0 / MSCALE, in1=max_hi[:, u, :],
                                                   op0=ALU.mult, op1=ALU.subtract).then_inc(lo_made, 1)

                maxima(0, 0, False, grouped=False)
                nc.vector.memset(ones[:, :], 1.0)
                nc.vector.memset(k_exp[KROWS:XROWS, CPB // 2:, :, :], MSCALE).then_inc(ones_set, 1)
                maxima(1, 1, False)
                with dve.Fori(1, UNITS // 2) as i:
                    maxima(i * 2, 0, True)
                    maxima(i * 2 + 1, 1, True)
                invert(UNITS - 2)
                for piece in range(len(DVE_ADDS_AT)):
                    add(UNITS - 1, 1, piece)
                invert(UNITS - 1)

            @block.gpsimd
            def _(pool):
                pool.sem_inc(on_pool, ADDS)
                nc.gpsimd.memset(k_exp[KROWS:XROWS, 0:CPB // 2, :, :], MSCALE).then_inc(ones_set, 1)
                pool.sem_inc(divided, 2)

                def divide(v, v2, u):
                    pool.wait_ge(o_read, v + 3)
                    pool.wait_ge(inv_in, v * (HQ * 16) + HQ * 16)
                    pool.wait_ge(stored[u], v2 * 16 + 16)
                    nc.gpsimd.tensor_tensor(a_sb[:, u, :], o_sb[:, u, :], inv_sb[:, u, :], ALU.mult).then_inc(divided, 1)

                def unit(v, v2, u, before):
                    pool.wait_ge(d_done, v + 1)
                    for n, s in enumerate(ON_POOL[1:]):
                        pool.wait_ge(p_ready, v * EXPS + (FREE_EX + HQ * (s + 1)))
                        a = probs[:, ON_POOL[0] + u * STEPS % RP, :, :] if n == 0 else acc[:, u, :, :]
                        if n:
                            pool.wait_ge(on_pool, v * ADDS + (ADDS + n))
                        nc.gpsimd.tensor_tensor(acc[:, u, :, :], a, probs[:, (u * STEPS + s) % RP, :, :], ALU.add).then_inc(on_pool, 1)
                        if n == DIVIDE_AT and before:
                            divide(v - 1, v2 - (1 - u), 1 - u)

                unit(0, 0, 0, False)
                unit(1, 0, 1, True)
                with pool.Fori(1, UNITS // 2) as i:
                    unit(i * 2, i, 0, True)
                    unit(i * 2 + 1, i, 1, True)
                divide(UNITS - 1, UNITS // 2 - 1, 1)

            @block.scalar
            def _(act):
                act.sem_inc(p_ready, FREE_EX)
                act.sem_inc(o_read, 2)
                act.sem_inc(d_read, 1)

                def read_o(v, u):
                    act.wait_ge(pv_done, v * STEPS + (FREE_PV + STEPS))
                    act.wait_ge(divided, v + 1)
                    nc.scalar.activation(o_sb[:, u, :], o_ps[:, :], ACT.Copy).then_inc(o_read, 1)

                def read_d(v, u):
                    act.wait_ge(d_done, v + 3)
                    act.wait_ge(inverted, v + 1)
                    nc.scalar.activation(d_sb[:, u, :], d_ps[:, :], ACT.Copy).then_inc(d_read, 1)

                def unit(v, u, before):
                    for s in range(STEPS):
                        for h in range(HQ):
                            n = HQ * s + h
                            if n == READ_SUMS_AT and before:
                                read_o(v - 1, 1 - u)
                            if n == READ_DENOMINATORS_AT and before:
                                read_d(v - 1, 1 - u)
                            if h == 0:
                                old = s - RP
                                act.wait_ge(pv_done, v * STEPS + (FREE_PV + old + 1))
                                back, at = (1, old + STEPS) if old < 0 else (0, old)
                                if at in ON_DVE:
                                    act.wait_ge(on_dve, v * len(DVE_ADDS_AT) + (len(DVE_ADDS_AT) * (1 - back) + 2 * max(ON_DVE.index(at), 1)))
                                elif at in ON_PE:
                                    act.wait_ge(on_pe, v * len(ON_PE) + (len(ON_PE) * (1 - back) + ON_PE.index(at) + 1))
                                else:
                                    act.wait_ge(on_pool, v * ADDS + (ADDS * (1 - back) + max(ON_POOL.index(at), 1)))
                            act.wait_ge(ex_done, v * EXPS + (n + 1))
                            nc.scalar.activation(probs[:, (u * STEPS + s) % RP, h, :], ex[n % 2][:, :], ACT.Exp, scale=SCALE).then_inc(p_ready, 1)

                unit(0, 0, False)
                unit(1, 1, True)
                with act.Fori(1, UNITS // 2) as i:
                    unit(i * 2, 0, True)
                    unit(i * 2 + 1, 1, True)
                read_o(UNITS - 1, 1)
                read_d(UNITS - 1, 1)

            @block.tensor
            def _(pe):
                pe.sem_inc(pv_done, FREE_PV)
                pe.sem_inc(mx_done, GR)
                pe.sem_inc(on_pe, len(ON_PE))
                pe.sem_inc(d_done, 2)

                def max_group(v, v2, v4, u, n):
                    if n == 0:
                        pe.wait_ge(qmax_in[u], (v2 + 1) * (3 * 16))
                    if n % (2 * QT) == 0:
                        pe.wait_ge(kmax_in[n // (2 * QT)], (v4 + 1) * (3 * 16))
                    if n != 1:
                        pe.wait_ge(mx_read, v * GR + (FREE_GR + n - 1 if n else FREE_GR))
                    else:
                        pe.wait_ge(lo_made, v)
                    scores_for_maxima(nc, g, mx[(u * (GR + 1) + n) % 2], u, n).then_inc(mx_done, 1)

                def turn_rows(v, u):
                    pe.wait_ge(row_ready, v + 1)
                    bank = mx[(u * (GR + 1) + GR) % 2]
                    nc.tensor.transpose(bank[0:HQ * QT, 0:P], row_max[:, :], ident[:, :]).then_inc(row_turned, 1)

                def scores(v, u, s, h):
                    n = HQ * s + h
                    pe.wait_ge(p_ready, v * EXPS + (n + 1))
                    nc.tensor.matmul(ex[n % 2][:, :], k_exp[:, s // TT, h, s % TT * P:(s % TT + 1) * P], q_exp[:, u, h, :],
                                     start=True, stop=True).then_inc(ex_done, 1)

                def sums(v, u, s):
                    pe.wait_ge(p_ready, v * EXPS + (FREE_EX + HQ * (s + 1)))
                    if s == 0:
                        pe.wait_ge(o_read, v + 2)
                    for h in range(HQ):
                        last = nc.tensor.matmul(o_ps[h * DH:(h + 1) * DH, :], v_sb[:, s // TT, s % TT, h * DH:(h + 1) * DH],
                                                probs[:, (u * STEPS + s) % RP, h, :], start=(s == 0), stop=(s == STEPS - 1))
                    last.then_inc(pv_done, 1)

                def add_up(v, u, s):
                    if s == ON_PE[0]:
                        pe.wait_ge(d_read, v + 1)
                    if s == "sum":
                        pe.wait_ge(on_dve, v * len(DVE_ADDS_AT) + 2 * len(DVE_ADDS_AT))
                    else:
                        pe.wait_ge(p_ready, v * EXPS + (FREE_EX + HQ * (s + 1)))
                    weights = dve_acc if s == "sum" else probs[:, (u * STEPS + s) % RP, :, :]
                    for h in range(HQ):
                        last = nc.tensor.matmul(d_ps[h * DH:(h + 1) * DH, :], ones[:, :], weights[:, h, :],
                                                start=(s == ON_PE[0]), stop=False)
                    last.then_inc(on_pe, 1)

                def close(v, u):
                    pe.wait_ge(on_pool, v * ADDS + 2 * ADDS)
                    for h in range(HQ):
                        last = nc.tensor.matmul(d_ps[h * DH:(h + 1) * DH, :], ones[:, :], acc[:, u, h, :], start=False, stop=True)
                    last.then_inc(d_done, 1)

                def unit(v, v2, v4, w2, w4, u, before, after):
                    n_scores = n_groups = n_sums = n_adds = 0
                    for work in ORDER:
                        if work == "S":
                            s, h = divmod(n_scores, HQ)
                            if n_scores == 0:
                                pe.wait_ge(qexp_in[u], (v2 + 1) * (3 * 16))
                                pe.wait_ge(rows_in[u], (v2 + 1) * (2 * 16))
                            if n_scores % (EXPS // 2) == 0:
                                pe.wait_ge(kv_in[s // (STEPS // 2)], (v4 + 1) * (8 * 16))
                            scores(v, u, s, h)
                            n_scores += 1
                        elif work == "G":
                            if after:
                                max_group(v + 1, w2, w4, 1 - u, n_groups)
                            n_groups += 1
                        elif work == "V":
                            if n_sums:
                                sums(v, u, n_sums - 1)
                            elif before:
                                sums(v - 1, 1 - u, STEPS - 1)
                            n_sums += 1
                        elif work == "A":
                            if n_adds:
                                add_up(v, u, ON_PE[n_adds - 1])
                            elif before:
                                add_up(v - 1, 1 - u, ON_PE[-1])
                            n_adds += 1
                        elif work == "C" and before:
                            close(v - 1, 1 - u)
                        elif work == "T" and after:
                            turn_rows(v + 1, 1 - u)

                def pair(i, before=True, after=True):
                    v = i * 2
                    unit(v, i, v // CPB, i, (v + 1) // CPB, 0, before, True)
                    unit(v + 1, i, (v + 1) // CPB, i + 1, (v + 2) // CPB, 1, True, after)

                turn_rows(0, 0)
                pe.wait_ge(ones_set, 2)
                pair(0, before=False)
                with pe.Fori(1, UNITS // 2 - 1) as i:
                    pair(i)
                pair(UNITS // 2 - 1, after=False)
                sums(UNITS - 1, 1, STEPS - 1)
                add_up(UNITS - 1, 1, ON_PE[-1])
                close(UNITS - 1, 1)


def finish_rows(nc, g):
    B, CPB, QUADS, D, NCH = (g[k] for k in ("B", "CPB", "QUADS", "D", "NCH"))
    TT = CH // P
    PAIRS = NCH // 2
    PRODUCTS = [(0, 0), (0, 1), (1, 0)]
    out_w, b_out_sb, out_scale = g["out_w"], g["b_out_sb"], g["out_scale"]
    with ExitStack() as ctx:
        def sb(name, shape, dt):
            return ctx.enter_context(nc.sbuf_tensor(name, shape, dt))

        def sem(name):
            return ctx.enter_context(nc.semaphore(name))

        a_in = sb("a_in", [P, 2, QUADS, CH], F32)
        a_halves = sb("a_halves", [P, 2, 2, QUADS, CH], F16)
        base_in = sb("base_in", [P, 2, TT, D], F32)
        o_out = sb("o_out", [P, 2, TT, D], F32)
        prod = [ctx.enter_context(nc.psum_tensor(f"prod{t}", [P, D], F32)) for t in range(TT)]
        a_loaded = [sem(f"a_loaded{u}") for u in range(2)]
        base_loaded = [sem(f"base_loaded{u}") for u in range(2)]
        out_stored = [sem(f"out_stored{u}") for u in range(2)]
        a_high = sem("a_high")
        a_split = sem("a_split")
        biased = sem("biased")
        multiplied = sem("multiplied")
        summed = sem("summed")

        with nc.Block() as block:
            @block.sync
            def _(sp):
                for s in out_stored:
                    sp.sem_inc(s, 16)
                a_view = g["a_dram"].rearrange("(b q c) p t -> b c p q t", b=B, q=QUADS)
                base_view = g["base_dram"].rearrange("(b c t p) d -> b c p t d", b=B, c=CPB, t=TT)
                with sp.Fori(0, B) as b:
                    with sp.Fori(0, CPB // 2) as ci:
                        for u in range(2):
                            c = b * CPB + ci * 2 + u
                            ch = ci * 2 + u
                            sp.wait_ge(a_split, c + 1)
                            sp.dma_start(a_in[:, u, :, :], a_view[b, ch]).then_inc(a_loaded[u], 16)
                            sp.wait_ge(summed, c * TT + TT)
                            sp.dma_start(base_in[:, u, :, :], base_view[b, ch]).then_inc(base_loaded[u], 16)

            @block.scalar
            def _(act):
                view = g["out_rows"].rearrange("(i u t p) d -> i u p t d", u=2, t=TT, p=P)

                def high(c, c2, u):
                    act.wait_ge(a_loaded[u], (c2 + 1) * 16)
                    act.wait_ge(multiplied, c * TT + TT)
                    nc.scalar.activation(a_halves[:, u, 0, :, :], a_in[:, u, :, :], ACT.Copy).then_inc(a_high, 1)

                def store(c, c2, u):
                    act.wait_ge(summed, c * TT + 3 * TT)
                    act.dma_start(view[c2, u], o_out[:, u, :, :]).then_inc(out_stored[u], 16)

                high(0, 0, 0)
                with act.Fori(0, PAIRS - 1) as i:
                    high(i * 2 + 1, i, 1)
                    store(i * 2, i, 0)
                    high(i * 2 + 2, i + 1, 0)
                    store(i * 2 + 1, i, 1)
                high(NCH - 1, PAIRS - 1, 1)
                store(NCH - 2, PAIRS - 1, 0)
                store(NCH - 1, PAIRS - 1, 1)
                for s in out_stored:
                    act.wait_ge(s, 16 * (1 + NCH // 2))

            @block.gpsimd
            def _(pool):
                with pool.Fori(0, PAIRS) as i:
                    for u in range(2):
                        pool.wait_ge(base_loaded[u], i * 16 + 16)
                        nc.gpsimd.tensor_tensor(base_in[:, u, :, :], base_in[:, u, :, :],
                                                b_out_sb[:, :].unsqueeze(1).to_broadcast([P, TT, D]), ALU.add).then_inc(biased, 1)

            @block.tensor
            def _(pe):
                pe.sem_inc(multiplied, 2 * TT)
                with pe.Fori(0, PAIRS) as i:
                    for u in range(2):
                        pe.wait_ge(a_split, i * 2 + (u + 3))
                        for t in range(TT):
                            pe.wait_ge(summed, (i * 2 + u) * TT + (t + 1 + TT))
                            for q in range(QUADS):
                                for a, b in PRODUCTS:
                                    last = nc.tensor.matmul(prod[t][:, :], a_halves[:, u, a, q, t * P:(t + 1) * P], out_w[:, b, q, :],
                                                            start=(q == a == b == 0), stop=(q == QUADS - 1 and a == 1))
                            last.then_inc(multiplied, 1)

            @block.vector
            def _(dve):
                dve.sem_inc(summed, 2 * TT)
                dve.sem_inc(a_split, 2)

                def low(c, u):
                    dve.wait_ge(a_high, c + 1)
                    nc.vector.tensor_tensor(a_halves[:, u, 1, :, :], a_in[:, u, :, :], a_halves[:, u, 0, :, :], ALU.subtract).then_inc(a_split, 1)

                def chunk(c, c2, u, more):
                    dve.wait_ge(biased, c + 1)
                    dve.wait_ge(out_stored[u], c2 * 16 + 16)
                    for t in range(TT):
                        if t == 1 and more:
                            low(c + 1, 1 - u)
                        dve.wait_ge(multiplied, c * TT + (t + 1 + 2 * TT))
                        nc.vector.scalar_tensor_tensor(out=o_out[:, u, t, :], in0=prod[t][:, :], scalar=out_scale[:, 0:1],
                                                       in1=base_in[:, u, t, :], op0=ALU.mult, op1=ALU.add).then_inc(summed, 1)

                low(0, 0)
                with dve.Fori(0, PAIRS - 1) as i:
                    chunk(i * 2, i, 0, True)
                    chunk(i * 2 + 1, i, 1, True)
                chunk(NCH - 2, PAIRS - 1, 0, True)
                chunk(NCH - 1, PAIRS - 1, 1, False)


_INS = ["L0_attn_x", "L0_attn_w_qkv", "L0_attn_w_out", "L0_attn_b_out", "L0_attn_mask_logits",
        "L0_ffn_w_gate", "L0_ffn_w_expert", "L0_ffn_b_expert"]


def _constants(tokens):
    import numpy as np
    dh, heads = 32, 4
    n = np.arange(dh)
    rows = [np.sqrt((1.0 if f in (0, dh // 2) else 2.0) / dh) * np.cos(2 * np.pi * f * n / dh) for f in range(dh // 2 + 1)]
    rows += [np.sqrt(2.0 / dh) * np.sin(2 * np.pi * f * n / dh) for f in range(1, dh // 2)]
    basis = np.kron(np.eye(heads), np.stack(rows)).astype(np.float32)
    prefix = np.triu(np.ones((P, P))).astype(np.float32)
    rank = np.tile(np.arange(EXPERTS, 0, -1), (P, 1)).astype(np.float32)
    token = np.zeros((P, 2, tokens // P), np.float32)
    token[:, 0] = np.arange(tokens // P) * P
    token[:, 1] = np.arange(1, P + 1)[:, None]
    place = np.tile(np.arange(1, CAPACITY + 1), (P, 1)).astype(np.float32)
    return {"ident": np.eye(P, dtype=np.float32), "basis": basis, "prefix": prefix, "rank": rank,
            "token": token, "place": place}


def kernel(**inputs):
    import numpy as np
    import concourse.bacc as bacc
    from concourse.bass_utils import run_bass_kernel_spmd

    nc = bacc.Bacc("TRN2", target_bir_lowering=False, num_devices=1)
    arrays, args = {}, []
    for name, a in [(n, inputs[n]) for n in _INS] + list(_constants(inputs["L0_attn_x"].shape[0] * inputs["L0_attn_x"].shape[1]).items()):
        a = np.ascontiguousarray(a)
        arrays[f"in_{name}"] = a
        args.append(nc.dram_tensor(f"in_{name}", a.shape, mybir.dt.from_np(a.dtype), kind="ExternalInput").ap())
    out = nc.dram_tensor("out_0", inputs["L0_attn_x"].shape, F32, kind="ExternalOutput").ap()
    attention_and_experts_kernel(nc, *args, out)
    r = run_bass_kernel_spmd(nc, [arrays], core_ids=[0])
    return r.results[0]["out_0"]
```
